# Optimizing a Trainium2 kernel written in Bass

```python
import numpy as np
import jax
import jax.numpy as jnp

def _softmax(x, axis=-1):
    return jax.nn.softmax(x, axis=axis)

def _gelu(x):
    return jax.nn.gelu(x, approximate=True)

def _silu(x):
    return jax.nn.silu(x)

def _sigmoid(x):
    return jax.nn.sigmoid(x)

def _layernorm(x, axis=-1, eps=1e-05):
    m = jnp.mean(x, axis=axis, keepdims=True)
    v = jnp.var(x, axis=axis, keepdims=True)
    return (x - m) / jnp.sqrt(v + eps)

def _scatter_add(tgt, idx, src, axis=0):
    return tgt.at[idx].add(src)

def _segment_sum(src, seg, n):
    return jax.ops.segment_sum(src, seg, n)
kernel_name = 'mk_gps_d1_gnn_r8_108fdd'

def setup_inputs(seed: int=0):
    np.random.seed(seed)
    _w = jnp.asarray

    def _rec_inputs():
        import jax
        import jax.numpy as jnp
        _gk = jax.random.key(seed)
        x = -6.415e-05 + 1 * jax.random.normal(jax.random.fold_in(_gk, 1), (1250, 512), jnp.float32)
        src = jax.random.randint(jax.random.fold_in(_gk, 2), (20000,), 0, 1250, jnp.int32)
        dst = jax.random.randint(jax.random.fold_in(_gk, 3), (20000,), 0, 1250, jnp.int32)
        _o = jnp.argsort(dst, stable=True)
        src = src[_o]
        dst = dst[_o]
        return (x, src, dst)
    x, src, dst = _rec_inputs()

    def _L0_gnn_setup():
        import jax, jax.numpy as jnp
        import numpy as np
        N_NODES = 2500
        N_EDGES = 20000
        D = 512
        L = 4
        NEG_SLOPE = 0.01
        key = jax.random.key(seed)
        k_x, k_e, k_w = jax.random.split(key, 3)
        x = jax.random.normal(k_x, (N_NODES, D), dtype=jnp.float32)
        edge_index = jax.random.randint(k_e, (2, N_EDGES), 0, N_NODES, dtype=jnp.int64)
        limit = np.sqrt(6.0 / (D + D)).astype(np.float32)
        Ws = jax.random.uniform(k_w, (L, D, D), dtype=jnp.float32, minval=-limit, maxval=limit)
        bs = jnp.zeros((L, D), dtype=jnp.float32)
        return {'x': x, 'edge_index': edge_index, 'Ws': Ws, 'bs': bs}
    _L0_gnn_all = _L0_gnn_setup()
    _L0_gnn_in = {k: v for k, v in _L0_gnn_all.items() if k in ('Ws', 'bs')}
    del _L0_gnn_all

    def _L0_mix_setup():
        import jax, jax.numpy as jnp
        import numpy as np
        DIM = 512
        HEADS = 8

        def _reference_tuple_inner(x, Wqkv, temperature, Wproj, bproj):
            B, N, C = x.shape
            H = temperature.shape[0]
            D = C // H
            qkv = (x @ Wqkv.T).reshape(B, N, 3, H, D).transpose(2, 0, 3, 1, 4)
            q, k, v = (qkv[0], qkv[1], qkv[2])
            q = jax.nn.relu(q)
            k = jax.nn.relu(k)
            ksum = k.sum(axis=2)
            denom = jnp.clip(jnp.einsum('bhnd,bhd->bhn', q, ksum), 100.0)[..., None]
            attn = jnp.einsum('bhnd,bhne->bhde', k, v) * temperature
            attn1 = jnp.einsum('bhnd,bhde->bhne', q, attn)
            out = attn1 / denom
            y = out.transpose(0, 2, 1, 3).reshape(B, N, C) @ Wproj.T + bproj
            return (y, attn1)
        key = jax.random.key(seed)
        k1, k2, k3, k4 = jax.random.split(key, 4)
        head_dim = DIM // HEADS
        scale = head_dim ** (-0.5)
        x = jax.random.normal(k1, (4, 512, DIM), dtype=jnp.float32)
        Wqkv = jax.random.normal(k2, (3 * DIM, DIM), dtype=jnp.float32) * DIM ** (-0.5)
        temperature = jnp.ones((HEADS, 1, 1), dtype=jnp.float32) * scale
        Wproj = jax.random.normal(k3, (DIM, DIM), dtype=jnp.float32) * DIM ** (-0.5)
        bproj = jnp.zeros((DIM,), dtype=jnp.float32)
        return {'x': x, 'Wqkv': Wqkv, 'temperature': temperature, 'Wproj': Wproj, 'bproj': bproj}
    _L0_mix_all = _L0_mix_setup()
    _L0_mix_in = {k: v for k, v in _L0_mix_all.items() if k in ('Wqkv', 'temperature', 'Wproj', 'bproj')}
    del _L0_mix_all

    def _L0_ffn_setup():
        import jax, jax.numpy as jnp
        import numpy as np
        from jax import lax
        N_HEADS = 8
        D_KEYS = 128
        HALF = D_KEYS // 2
        N_KEYS = 256
        TOP_K = 8
        D_MODEL = 512

        def _forward(queries, Wq, bq, keys, w_down, w_up):
            N, T, D = queries.shape
            x = queries.reshape(-1, D)
            q = (x @ Wq + bq).reshape(-1, N_HEADS, D_KEYS)
            q1, q2 = (q[..., :HALF], q[..., HALF:])
            s1 = jnp.einsum('bhc,hnc->bhn', q1, keys[:, 0])
            s2 = jnp.einsum('bhc,hnc->bhn', q2, keys[:, 1])
            s1t, i1 = lax.top_k(s1, TOP_K)
            s2t, i2 = lax.top_k(s2, TOP_K)
            all_scores = (s1t[..., :, None] + s2t[..., None, :]).reshape(-1, N_HEADS, TOP_K * TOP_K)
            all_idx = (i1[..., :, None] * N_KEYS + i2[..., None, :]).reshape(-1, N_HEADS, TOP_K * TOP_K)
            scores, best = lax.top_k(all_scores, TOP_K)
            indices = jnp.take_along_axis(all_idx, best, axis=-1)
            w_d = w_down[indices]
            w_u = w_up[indices]
            inner = jnp.einsum('bd,bhkd->bhk', x, w_d)
            vals = jax.nn.relu(inner) * jax.nn.softmax(scores, axis=-1)
            out = jnp.einsum('bhk,bhkd->bd', vals, w_u)
            return out.reshape(N, T, D)
        key = jax.random.key(seed)
        ks = jax.random.split(key, 6)
        N, T = (2, 1024)
        queries = jax.random.normal(ks[0], (N, T, D_MODEL), dtype=jnp.float32)
        Wq = jax.random.normal(ks[1], (D_MODEL, N_HEADS * D_KEYS), dtype=jnp.float32) / np.sqrt(D_MODEL)
        bq = jnp.zeros((N_HEADS * D_KEYS,), dtype=jnp.float32)
        bound = 1.0 / np.sqrt(HALF)
        keys = jax.random.uniform(ks[2], (N_HEADS, 2, N_KEYS, HALF), dtype=jnp.float32, minval=-bound, maxval=bound)
        w_down = jax.random.normal(ks[3], (N_KEYS * N_KEYS, D_MODEL), dtype=jnp.float32) * 0.02
        w_up = jax.random.normal(ks[4], (N_KEYS * N_KEYS, D_MODEL), dtype=jnp.float32) * 0.02
        return {'queries': queries, 'Wq': Wq, 'bq': bq, 'keys': keys, 'w_down': w_down, 'w_up': w_up}
    _L0_ffn_all = _L0_ffn_setup()
    _L0_ffn_in = {k: v for k, v in _L0_ffn_all.items() if k in ('Wq', 'bq', 'keys', 'w_down', 'w_up')}
    del _L0_ffn_all
    return {'x': x, 'src': src, 'dst': dst, 'L0_gnn_Ws': _L0_gnn_in['Ws'], 'L0_gnn_bs': _L0_gnn_in['bs'], 'L0_mix_Wqkv': _L0_mix_in['Wqkv'], 'L0_mix_temperature': _L0_mix_in['temperature'], 'L0_mix_Wproj': _L0_mix_in['Wproj'], 'L0_mix_bproj': _L0_mix_in['bproj'], 'L0_ffn_Wq': _L0_ffn_in['Wq'], 'L0_ffn_bq': _L0_ffn_in['bq'], 'L0_ffn_keys': _L0_ffn_in['keys'], 'L0_ffn_w_down': _L0_ffn_in['w_down'], 'L0_ffn_w_up': _L0_ffn_in['w_up']}

def reference(x, src, dst, L0_gnn_Ws, L0_gnn_bs, L0_mix_Wqkv, L0_mix_temperature, L0_mix_Wproj, L0_mix_bproj, L0_ffn_Wq, L0_ffn_bq, L0_ffn_keys, L0_ffn_w_down, L0_ffn_w_up):
    import jax
    import jax.numpy as jnp

    def _L0_gnn_ref(x, edge_index, Ws, bs):
        import jax, jax.numpy as jnp
        import numpy as np
        N_NODES = 2500
        N_EDGES = 20000
        D = 512
        L = 4
        NEG_SLOPE = 0.01
        'Stack of GCNConv (add self-loops, symmetric norm) + LeakyReLU per layer.'
        n = x.shape[0]
        loops = jnp.arange(n, dtype=edge_index.dtype)
        row = jnp.concatenate([edge_index[0], loops])
        col = jnp.concatenate([edge_index[1], loops])
        deg = jax.ops.segment_sum(jnp.ones_like(col, dtype=x.dtype), col, num_segments=n)
        dinv = jnp.where(deg > 0, jax.lax.rsqrt(deg), 0.0)
        norm = (dinv[row] * dinv[col])[:, None]
        for l in range(Ws.shape[0]):
            h = x @ Ws[l]
            msg = h[row] * norm
            agg = jax.ops.segment_sum(msg, col, num_segments=n)
            x = jax.nn.leaky_relu(agg + bs[l], NEG_SLOPE)
        return x

    def _L0_mix_ref(x, Wqkv, temperature, Wproj, bproj):
        import jax, jax.numpy as jnp
        import numpy as np
        DIM = 512
        HEADS = 8

        def _reference_tuple_inner(x, Wqkv, temperature, Wproj, bproj):
            B, N, C = x.shape
            H = temperature.shape[0]
            D = C // H
            qkv = (x @ Wqkv.T).reshape(B, N, 3, H, D).transpose(2, 0, 3, 1, 4)
            q, k, v = (qkv[0], qkv[1], qkv[2])
            q = jax.nn.relu(q)
            k = jax.nn.relu(k)
            ksum = k.sum(axis=2)
            denom = jnp.clip(jnp.einsum('bhnd,bhd->bhn', q, ksum), 100.0)[..., None]
            attn = jnp.einsum('bhnd,bhne->bhde', k, v) * temperature
            attn1 = jnp.einsum('bhnd,bhde->bhne', q, attn)
            out = attn1 / denom
            y = out.transpose(0, 2, 1, 3).reshape(B, N, C) @ Wproj.T + bproj
            return (y, attn1)
        return _reference_tuple_inner(x, Wqkv, temperature, Wproj, bproj)[0]

    def _L0_ffn_ref(queries, Wq, bq, keys, w_down, w_up):
        import jax, jax.numpy as jnp
        import numpy as np
        from jax import lax
        N_HEADS = 8
        D_KEYS = 128
        HALF = D_KEYS // 2
        N_KEYS = 256
        TOP_K = 8
        D_MODEL = 512

        def _forward(queries, Wq, bq, keys, w_down, w_up):
            N, T, D = queries.shape
            x = queries.reshape(-1, D)
            q = (x @ Wq + bq).reshape(-1, N_HEADS, D_KEYS)
            q1, q2 = (q[..., :HALF], q[..., HALF:])
            s1 = jnp.einsum('bhc,hnc->bhn', q1, keys[:, 0])
            s2 = jnp.einsum('bhc,hnc->bhn', q2, keys[:, 1])
            s1t, i1 = lax.top_k(s1, TOP_K)
            s2t, i2 = lax.top_k(s2, TOP_K)
            all_scores = (s1t[..., :, None] + s2t[..., None, :]).reshape(-1, N_HEADS, TOP_K * TOP_K)
            all_idx = (i1[..., :, None] * N_KEYS + i2[..., None, :]).reshape(-1, N_HEADS, TOP_K * TOP_K)
            scores, best = lax.top_k(all_scores, TOP_K)
            indices = jnp.take_along_axis(all_idx, best, axis=-1)
            w_d = w_down[indices]
            w_u = w_up[indices]
            inner = jnp.einsum('bd,bhkd->bhk', x, w_d)
            vals = jax.nn.relu(inner) * jax.nn.softmax(scores, axis=-1)
            out = jnp.einsum('bhk,bhkd->bd', vals, w_u)
            return out.reshape(N, T, D)
        return _forward(queries, Wq, bq, keys, w_down, w_up)
    edge_index = jnp.stack([src, dst])
    xn = _layernorm(x, axis=-1)
    x = x + _L0_gnn_ref(xn, edge_index, L0_gnn_Ws, L0_gnn_bs) + _L0_mix_ref(xn[None], L0_mix_Wqkv, L0_mix_temperature, L0_mix_Wproj, L0_mix_bproj)[0]
    x = x + _L0_ffn_ref(_layernorm(x, axis=-1)[None], L0_ffn_Wq, L0_ffn_bq, L0_ffn_keys, L0_ffn_w_down, L0_ffn_w_up)[0]
    return x

_drawn_inputs = setup_inputs


def setup_inputs(seed=0):
    import zlib

    import numpy as np

    out = dict(_drawn_inputs(seed))
    spreads = {'L0_gnn_bs': (0.0, 0.1),
     'L0_mix_temperature': (0.125, 0.6),
     'L0_mix_bproj': (0.0, 0.1),
     'L0_ffn_bq': (0.0, 0.8)}
    factors = {'L0_mix_Wqkv': 8.0,
     'L0_mix_Wproj': 8.0,
     'L0_ffn_Wq': 8.0,
     'L0_ffn_keys': 8.0,
     'L0_ffn_w_down': 8.0,
     'L0_ffn_w_up': 8.0}
    for name, (base, spread) in spreads.items():
        noise = np.random.default_rng([zlib.crc32(name.encode()), seed]).standard_normal(out[name].shape)
        drawn = base * np.exp(spread * noise) if base else spread * noise
        out[name] = jnp.asarray(drawn.astype(out[name].dtype))
    for name, factor in factors.items():
        out[name] = (out[name] * factor).astype(out[name].dtype)
    return out
```

```python
import numpy as np
from contextlib import ExitStack

import concourse.bass as bass
from concourse import mybir

ALU = mybir.AluOpType
ACT = mybir.ActivationFunctionType
AX = mybir.AxisListType
F32 = mybir.dt.float32
F16 = mybir.dt.float16
I32 = mybir.dt.int32
U32 = mybir.dt.uint32

N = 1250
D = 512
E = 20000
TP = 125
NT = N // TP
EB = 125
NP = E // (2 * EB)
KC = D // 128
L = 4
H = 8
NK = 256
TOPK = 8
COLS = [(0, 418), (418, 416), (834, 416)]
SLOPE = 0.01
EPS = 1e-5
DEN_MIN = 100.0
SLOTS = 16
FT = 128
CHUNKS = [(c, n) for c in range(KC) for n in range(len(COLS))]


def gps_block(nc, x, src, dst, Ws, bs, WqkvT, temperature, WprojT, bproj, Wq, bq, keysT, table, out):
    with ExitStack() as ctx:
        base = [16512]

        def at(name, shape, dt, offset):
            return nc.alloc_sbuf_tensor_at(name, shape, dt, offset=offset)

        def region(nbytes):
            o = base[0]
            base[0] += (nbytes + 31) // 32 * 32
            return o

        def carve(start, *specs):
            made, o = [], start
            for name, shape, dt in specs:
                made.append(at(name, shape, dt, o))
                size = int(np.prod(shape[1:])) * (2 if dt == F16 else 4)
                o += (size + 31) // 32 * 32
            carve.end = o
            return made

        def sem(name):
            return ctx.enter_context(nc.semaphore(name))

        r_ct, r_h, r_xt, r_w = region(50000), region(20480), region(20000), region(8192)
        r_ring, r_x1, r_misc, r_small = region(65536), region(20480), region(23328), region(3000)

        CT, = carve(r_ct, ("CT", [128, NT, N], F32))
        hP, = carve(r_h, ("hP", [128, NT, D], F32))
        xn, = carve(r_h, ("xn", [128, NT, D], F32))
        outT, = carve(r_h, ("outT", [128, KC, N], F32))
        xT, = carve(r_xt, ("xT", [128, KC, N], F32))
        W, = carve(r_w, ("W", [128, KC, D], F32))
        x1, = carve(r_x1, ("x1", [128, NT, D], F32))
        wqkv, wproj, qT, k_sb, v_sb, attnBD, ksumBD = carve(
            r_ring, ("wqkv", [128, KC, 3 * D], F32), ("wproj", [128, KC, D], F32), ("qT", [128, KC, N], F32),
            ("k_sb", [128, 2, D], F32), ("v_sb", [128, 2, KC, 132], F32),
            ("attnBD", [128, KC, 128], F32), ("ksumBD", [128, KC, 128], F32))
        assert carve.end <= r_x1
        iota_row, Eye, oh_src, oh_dst, edge_i, edge_f = carve(
            r_misc, ("iota_row", [128, N], F16), ("Eye", [128, 19 * TP], F16),
            ("oh_src", [128, 2, N], F16), ("oh_dst", [128, 2, 128], F16),
            ("edge_i", [80, 2, 2 * EB], I32), ("edge_f", [80, 2, 2 * EB], F32))
        eye_i, = carve(r_h, ("eye_i", [128, 19 * TP], I32))
        deg_bc, newton, dinv_bc, z_sb = carve(
            r_misc, ("deg_bc", [128, N], F32), ("newton", [128, N], F32), ("dinv_bc", [128, N], F32),
            ("z_sb", [128, 2, 512], F32))
        assert carve.end <= r_small
        b_row, bproj_row = carve(r_misc + 19200, ("b_row", [128, D], F32), ("bproj_row", [128, D], F32))
        assert carve.end <= r_small
        (edgeT, ident, ones, b_col, temp_col, stats, mv, rstd, dinv_col, mm, thr, ahead, upper, bnd,
         bounds, iota8) = carve(
            r_small - 0, ("edgeT", [128, 2, 2, NP], F32), ("ident", [128, 128], F32), ("ones", [128, 128], F32),
            ("b_col", [128, L, KC], F32), ("temp_col", [128, KC], F32), ("stats", [128, NT, 6], F32),
            ("mv", [128, NT, 2], F32), ("rstd", [128, 2, NT], F32), ("dinv_col", [128, NT], F32),
            ("mm", [80, 2], F32), ("thr", [16, 2], F32),
            ("ahead", [16, NT], F32), ("upper", [16, 2, NT], F32), ("bnd", [16, 4], F32), ("bounds", [1, 3, NT], I32),
            ("iota8", [128, 8], F32))
        assert carve.end <= 229368, carve.end
        diag_mm, iota80, bnd_hit = carve(r_h + 12000, ("diag_mm", [80, 2, NP], F32), ("iota80", [16, 2, NP], F32),
                                         ("bnd_hit", [16, 2, NP], F32))

        (xl, xlT, qh, v8, i8, sums, pick, best8, pos8, pos_ab, g12, e8, p8, inner, vals, idx, bq_col, esum,
         prod, y_sb, fstats) = carve(
            r_ct, ("xl", [128, 2, D], F32), ("xlT", [128, KC, 128], F32), ("qh", [128, H, 128], F32),
            ("v8", [128, 2 * H, 8], F32), ("i8", [128, 2 * H, 8], U32), ("sums", [128, H, 64], F32),
            ("pick", [128, 64, 8], F32), ("best8", [128, H, 8], F32), ("pos8", [128, H, 8], U32),
            ("pos_ab", [128, 2, 64], U32), ("g12", [128, 2, 64], F32), ("e8", [128, H, 8], F32),
            ("p8", [128, 2, H, 8], F32), ("inner", [128, H, 8], F32), ("vals", [128, H, 8], F32),
            ("idx", [128, 2, H * 8], U32), ("bq_col", [128, H], F32), ("esum", [128, 2, H], F32),
            ("prod", [128, D], F32), ("y_sb", [128, 2, D], F32), ("fstats", [128, 16], F32))
        assert carve.end <= r_h
        diag, = carve(r_h, ("diag", [128, 2, 8, TP], F32))
        wq, = carve(r_xt, ("wq", [128, KC, 2 * D], F32))
        keys, = carve(r_w, ("keys", [128, H, NK], F32))
        ring, = carve(r_ring, ("ring", [128, SLOTS, 2 * D], F32))

        ps = ctx.enter_context(nc.psum_tensor("ps", [128, 8, 512], F32))

        x_loaded, edges_loaded, vec_loaded = sem("x_loaded"), sem("edges_loaded"), sem("vec_loaded")
        wqkv_loaded, wproj_loaded, w_loaded = sem("wqkv_loaded"), sem("wproj_loaded"), sem("w_loaded")
        rows_loaded = sem("rows_loaded")
        iotas_made, eye_made = sem("iotas_made"), sem("eye_made")
        dve_step = sem("dve_step")
        edges_float = sem("edges_float")
        edges_turned = sem("edges_turned")
        edgeT_ready, bnd_ready = sem("edgeT_ready"), sem("bnd_ready")
        bnd_rows, bounds_ready = sem("bnd_rows"), sem("bounds_ready")
        oh_ready = [sem(f"oh_ready{i}") for i in range(2)]
        oh_free = [sem(f"oh_free{i}") for i in range(2)]
        ct_full, ct_free = sem("ct_full"), sem("ct_free")
        stats_ready, std_ready, rstd_ready, xn_ready = (sem("stats_ready"), sem("std_ready"),
                                                        sem("rstd_ready"), sem("xn_ready"))
        xnT_full, xnT_done = sem("xnT_full"), sem("xnT_done")
        deg_full, deg_sqrt, dinv_ready = sem("deg_full"), sem("deg_sqrt"), sem("dinv_ready")
        kv_full, k_done, v_done, kvmm_done = sem("kv_full"), sem("k_done"), sem("v_done"), sem("kvmm_done")
        vones_ready, bd_zero, bd_ready = sem("vones_ready"), sem("bd_zero"), sem("bd_ready")
        q_full, q_done = sem("q_full"), sem("q_done")
        o_full, o_done, y_full, y_done = sem("o_full"), sem("o_done"), sem("y_full"), sem("y_done")
        h_full, h_done, agg_full, z_ready, zb_ready, xt_done = (
            sem("h_full"), sem("h_done"), sem("agg_full"), sem("z_ready"), sem("zb_ready"), sem("xt_done"))
        last_full, x1_done = sem("last_full"), sem("x1_done")
        f_mv, f_std, f_rstd, xl_done = sem("f_mv"), sem("f_std"), sem("f_rstd"), sem("xl_done")
        xlT_full, xlT_done, qh_full, qh_done = sem("xlT_full"), sem("xlT_done"), sem("qh_full"), sem("qh_done")
        s_full, s_done, shift_ready, exp_done = sem("s_full"), sem("s_done"), sem("shift_ready"), sem("exp_done")
        idx_ready, idx_zero = sem("idx_ready"), sem("idx_zero")
        gathered = [sem(f"gathered{i}") for i in range(SLOTS)]
        vals_ready, diag_ready, group_used = sem("vals_ready"), sem("diag_ready"), sem("group_used")
        y_left = sem("y_left")
        y_free = sem("y_free")
        out_stored = sem("out_stored")
        waited = sem("waited")
        wq_loaded = sem("wq_loaded")

        block = ctx.enter_context(nc.Block())

        def after(engine, signal, value):
            engine.wait_ge(signal, value)
            engine.nop().then_inc(waited, 1)

        def weights(w):
            return w.rearrange("(c p) n -> p c n", p=128)

        @block.sync
        def _(sp):
            sp.dma_start(edge_i[:, 0, :], dst.rearrange("(p e) -> p e", e=2 * EB)).then_inc(edges_loaded, 16)
            sp.dma_start(edge_i[:, 1, :], src.rearrange("(p e) -> p e", e=2 * EB)).then_inc(edges_loaded, 16)
            sp.dma_start(x1[0:TP], x.rearrange("(t p) d -> p t d", p=TP)).then_inc(x_loaded, 16)
            sp.dma_start(wqkv[:], weights(WqkvT)).then_inc(wqkv_loaded, 16)
            sp.dma_start(wproj[:], weights(WprojT)).then_inc(wproj_loaded, 16)
            sp.dma_start(W[:], weights(Ws[0])).then_inc(w_loaded, 16)
            with nc.allow_non_contiguous_dma("small vectors"):
                sp.dma_start(b_col[:], bs.rearrange("l (c p) -> p l c", p=128)).then_inc(vec_loaded, 16)
                for half in range(2):
                    t_half = temperature.rearrange("(c a) u v -> a (u v) c", a=2)[half]
                    sp.dma_start(temp_col[64 * half:64 * half + 64, :],
                                 t_half.to_broadcast([64, KC])).then_inc(vec_loaded, 16)
            sp.dma_start(b_row[0:TP], bs[L - 1:L, :].to_broadcast([TP, D])).then_inc(rows_loaded, 16)
            sp.dma_start(bproj_row[0:TP], bproj.rearrange("(a d) -> a d", a=1).to_broadcast([TP, D])
                         ).then_inc(rows_loaded, 16)
            for l in range(L - 1):
                sp.wait_ge(h_full, NT * (l + 1))
                sp.dma_start(W[:], weights(Ws[l + 1])).then_inc(w_loaded, 16)
            sp.wait_ge(h_full, NT * L)
            sp.dma_start(wq[:], weights(Wq)).then_inc(wq_loaded, 16)
            sp.dma_start(keys[:], keysT.rearrange("p (h n) -> p h n", h=H)).then_inc(wq_loaded, 16)
            sp.wait_ge(last_full, NT)
            with nc.allow_non_contiguous_dma("small vector"):
                sp.dma_start(bq_col[:], bq.rearrange("(h p) -> p h", p=128)).then_inc(wq_loaded, 16)

            sp.nop().then_inc(y_free, 2)
            with sp.Fori(0, NT // 2) as it:
                for par in range(2):
                    t = it * 2 + par
                    sp.wait_ge(y_left, t + 2)
                    sp.dma_start(out[bass.ds(it * (2 * TP) + par * TP, TP), :], y_sb[0:TP, par]
                                 ).then_inc(out_stored, 16)
                    sp.wait_ge(out_stored, (t + 1) * 16)
                    sp.nop().then_inc(y_free, 1)

        @block.gpsimd
        def _(pool):
            nc.gpsimd.iota(iota_row[:], [[1, N]], base=0, channel_multiplier=0,
                           allow_small_or_imprecise_dtypes=True)
            nc.gpsimd.iota(eye_i[:], [[1, 19 * TP]], base=-9 * TP, channel_multiplier=-1)
            nc.gpsimd.iota(iota80[0:NT, 0, :], [[1, NP]], base=1, channel_multiplier=0,
                           allow_small_or_imprecise_dtypes=True)
            nc.gpsimd.iota(iota80[0:NT, 1, :], [[-1, NP]], base=NP, channel_multiplier=0,
                           allow_small_or_imprecise_dtypes=True)
            nc.gpsimd.iota(thr[0:NT, 0:1], [[0, 1]], base=0, channel_multiplier=TP,
                           allow_small_or_imprecise_dtypes=True)
            nc.gpsimd.iota(thr[0:NT, 1:2], [[0, 1]], base=TP - 1, channel_multiplier=TP,
                           allow_small_or_imprecise_dtypes=True)
            nc.gpsimd.iota(ahead[0:NT, :], [[1, NT]], base=0, channel_multiplier=-1,
                           allow_small_or_imprecise_dtypes=True)
            nc.gpsimd.iota(iota8[:], [[1, 8]], base=0, channel_multiplier=0,
                           allow_small_or_imprecise_dtypes=True)
            nc.gpsimd.memset(ones[:], 1.0).then_inc(iotas_made, 1)
            nc.gpsimd.memset(attnBD[:], 0.0)
            nc.gpsimd.memset(ksumBD[:], 0.0).then_inc(bd_zero, 1)
            nc.gpsimd.memset(v_sb[:], 1.0).then_inc(vones_ready, 1)
            pool.wait_ge(last_full, NT)
            nc.gpsimd.memset(idx[:], 0).then_inc(idx_zero, 1)

            def gather_tile(it, par):
                t = it * 2 + par
                for g in range(H):
                    if g == 0:
                        pool.wait_ge(idx_ready, t + 1)
                    after(pool, group_used, t * H + g + 1)
                    for k in range(8):
                        slot = (g % 2) * 8 + k
                        nc.gpsimd.indirect_dma_start(
                            out=ring[:, slot, :], out_offset=None, in_=table,
                            in_offset=bass.IndirectOffsetOnAxis(ap=idx[:, par, 8 * g + k:8 * g + k + 1], axis=0),
                        ).then_inc(gathered[slot], 16)

            with pool.Fori(0, NT // 2) as it:
                for par in range(2):
                    gather_tile(it, par)

        @block.tensor
        def _(pe):
            mm_ = nc.tensor.matmul

            pe.wait_ge(eye_made, 1)
            pe.wait_ge(iotas_made, 1)
            pe.wait_ge(edges_float, 1)
            for k in range(2):
                for half in range(2):
                    nc.tensor.transpose(ps[0:EB, 0, (2 * k + half) * NP:(2 * k + half + 1) * NP],
                                        edge_f[:, k, half * EB:(half + 1) * EB], ident[0:NP, 0:NP])
            pe.wait_ge(edges_float, 2)
            mm_(ps[0:NT, 1, 0:2 * NP], ones[0:NP, 0:NT], diag_mm[:].rearrange("p a b -> p (a b)"),
                start=True, stop=True).then_inc(edges_turned, 1)
            pe.wait_ge(bnd_ready, 1)
            mm_(ps[0:1, 2, 0:NT], bnd[0:NT, 2:3], upper[0:NT, 0, :], start=True, stop=True)
            mm_(ps[0:1, 3, 0:NT], bnd[0:NT, 2:3], upper[0:NT, 1, :], start=True, stop=True)
            mm_(ps[0:1, 4, 0:NT], bnd[0:NT, 0:1], ident[0:NT, 0:NT], start=True, stop=False)
            mm_(ps[0:1, 4, 0:NT], bnd[0:NT, 3:4], upper[0:NT, 0, :], start=False, stop=True
                ).then_inc(bnd_rows, 1)

            pe.wait_ge(bounds_ready, 1)
            for half in range(2):
                pe.nop().then_inc(oh_free[half], 1)
            with pe.Fori(0, NT // 2) as jj:
                for par in range(2):
                    j = jj * 2 + par
                    first = pe.value_load(bounds[0:1, 0, bass.ds(j, 1)], min_val=0, max_val=NT * NP - 1)
                    end = pe.value_load(bounds[0:1, 1, bass.ds(j, 1)], min_val=1, max_val=NT * NP)
                    pe.wait_ge(ct_free, j + 1)
                    for b in range(3):
                        i0, ni = 4 * b, min(4, NT - 4 * b)
                        mm_(ps[0:TP, 3 * par + b, 0:ni * TP], Eye[0:TP, 9 * TP:10 * TP],
                            Eye[0:TP, bass.ds((9 + i0) * TP - j * TP, ni * TP)],
                            start=True, stop=False, skip_group_check=True)
                    with pe.Fori(first, end) as step:
                        for half in range(2):
                            pe.wait_ge(oh_ready[half], step + 1)
                            for i in range(NT):
                                last = mm_(ps[0:TP, 3 * par + i // 4, (i % 4) * TP:(i % 4 + 1) * TP],
                                           oh_src[0:EB, half, i * TP:(i + 1) * TP], oh_dst[0:EB, half, 0:TP],
                                           start=False, stop=False, skip_group_check=True)
                            last.then_inc(oh_free[half], 1)
                    pe.drain().then_inc(ct_full, 1)

            pe.wait_ge(ct_free, NT + 2)
            for n, (c0, w) in enumerate(COLS):
                for s in range(NT):
                    last = mm_(ps[:, n, 0:w], ones[0:TP, :], CT[0:TP, s, c0:c0 + w],
                               start=(s == 0), stop=(s == NT - 1))
            last.then_inc(deg_full, 1)

            for t in range(NT):
                pe.wait_ge(xn_ready, t + 1)
                if t >= 4:
                    pe.wait_ge(xnT_done, t - 3)
                for c in range(KC):
                    last = nc.tensor.transpose(ps[:, 4 + t % 4, c * TP:(c + 1) * TP],
                                               xn[0:TP, t, 128 * c:128 * c + 128], ident[0:TP, 0:TP])
                last.then_inc(xnT_full, 1)
            pe.wait_ge(xnT_done, NT)

            def kv_project(t):
                if t >= 2:
                    pe.wait_ge(k_done, t - 1)
                    pe.wait_ge(v_done, t - 1)
                for which in range(2):
                    for c in range(KC):
                        last = mm_(ps[0:TP, 2 * which + t % 2, :], xT[:, c, t * TP:(t + 1) * TP],
                                   wqkv[:, c, (1 + which) * D:(2 + which) * D], start=(c == 0), stop=(c == KC - 1))
                last.then_inc(kv_full, 1)

            def kv_outer(t):
                pe.wait_ge(k_done, t + 1)
                pe.wait_ge(v_done, t + 1)
                for c in range(KC):
                    last = mm_(ps[:, 4 + c, 0:129], k_sb[0:TP, t % 2, 128 * c:128 * c + 128],
                               v_sb[0:TP, t % 2, c, 0:129], start=(t == 0), stop=(t == NT - 1))
                last.then_inc(kvmm_done, 1)

            pe.wait_ge(wqkv_loaded, 16)
            pe.wait_ge(deg_sqrt, 1)
            kv_project(0)
            for t in range(1, NT):
                kv_project(t)
                kv_outer(t - 1)
            kv_outer(NT - 1)
            for i, (c, n) in enumerate(CHUNKS):
                c0, w = COLS[n]
                if i >= 4:
                    pe.wait_ge(q_done, i - 3)
                for k in range(KC):
                    last = mm_(ps[:, i % 4, 0:w], wqkv[:, k, 128 * c:128 * c + 128], xT[:, k, c0:c0 + w],
                               start=(k == 0), stop=(k == KC - 1))
                last.then_inc(q_full, 1)
            pe.wait_ge(bd_ready, 1)
            pe.wait_ge(q_done, len(CHUNKS))
            for i, (c, n) in enumerate(CHUNKS):
                c0, w = COLS[n]
                if i >= 2:
                    pe.wait_ge(o_done, i - 1)
                mm_(ps[:, 6 + i % 2, 0:w], ksumBD[:, c, :], qT[:, c, c0:c0 + w], start=True, stop=True)
                mm_(ps[:, 4 + i % 2, 0:w], attnBD[:, c, :], qT[:, c, c0:c0 + w], start=True, stop=True
                    ).then_inc(o_full, 1)
            pe.wait_ge(wproj_loaded, 16)
            pe.wait_ge(o_done, len(CHUNKS))
            for t in range(NT):
                if t >= 4:
                    pe.wait_ge(y_done, t - 3)
                for c in range(KC):
                    last = mm_(ps[0:TP, t % 4, :], outT[:, c, t * TP:(t + 1) * TP], wproj[:, c, :],
                               start=(c == 0), stop=(c == KC - 1))
                last.then_inc(y_full, 1)
            pe.wait_ge(y_done, NT)

            def layer_h(l):
                pe.wait_ge(w_loaded, l * 16 + 16)
                for t in range(NT):
                    if t >= 4:
                        pe.wait_ge(h_done, l * NT + t - 3)
                    for c in range(KC):
                        last = mm_(ps[0:TP, t % 4, :], xT[:, c, t * TP:(t + 1) * TP], W[:, c, :],
                                   start=(c == 0), stop=(c == KC - 1))
                    last.then_inc(h_full, 1)

            with pe.Fori(0, L - 1) as l:
                layer_h(l)
                pe.wait_ge(h_done, l * NT + NT)
                for i, (c, n) in enumerate(CHUNKS):
                    c0, w = COLS[n]
                    if i >= 4:
                        pe.wait_ge(z_ready, l * len(CHUNKS) + i - 3)
                    for s in range(NT):
                        last = mm_(ps[:, 4 + i % 4, 0:w], hP[0:TP, s, 128 * c:128 * c + 128],
                                   CT[0:TP, s, c0:c0 + w], start=(s == 0), stop=(s == NT - 1))
                    last.then_inc(agg_full, 1)
                pe.wait_ge(xt_done, l * len(CHUNKS) + len(CHUNKS))
            layer_h(L - 1)
            pe.wait_ge(h_done, L * NT)
            for t in range(NT):
                if t >= 4:
                    pe.wait_ge(x1_done, t - 3)
                for s in range(NT):
                    last = mm_(ps[0:TP, 4 + t % 4, :], CT[0:TP, s, t * TP:(t + 1) * TP], hP[0:TP, s, :],
                               start=(s == 0), stop=(s == NT - 1))
                last.then_inc(last_full, 1)

            def queries(t, par):
                pe.wait_ge(xl_done, t + 1)
                for c in range(KC):
                    last = nc.tensor.transpose(ps[:, 4, c * TP:(c + 1) * TP], xl[0:TP, par, 128 * c:128 * c + 128],
                                               ident[0:TP, 0:TP])
                last.then_inc(xlT_full, 1)
                pe.wait_ge(xlT_done, t + 1)
                for half in range(2):
                    for hh in range(4):
                        h = 4 * half + hh
                        for c in range(KC):
                            last = mm_(ps[:, 5 + half, hh * TP:(hh + 1) * TP], wq[:, c, 128 * h:128 * h + 128],
                                       xlT[:, c, 0:TP], start=(c == 0), stop=(c == KC - 1))
                    last.then_inc(qh_full, 1)

            def scores(t, h):
                pe.wait_ge(qh_done, t * 2 + h // 4 + 1)
                if h >= 2 or not isinstance(t, int) or t > 0:
                    pe.wait_ge(s_done, t * H + h - 1)
                for half in range(2):
                    last = mm_(ps[0:TP, 2 * (h % 2) + half, 0:NK], qh[64 * half:64 * half + 64, h, 0:TP],
                               keys[64 * half:64 * half + 64, h, :], start=True, stop=True)
                last.then_inc(s_full, 1)

            def weigh(t, g):
                if g == 0:
                    pe.wait_ge(y_left, t + 1)
                pe.wait_ge(diag_ready, t * H + g + 1)
                for k in range(8):
                    last = mm_(ps[0:TP, 7, :], diag[0:TP, g % 2, k, :], ring[0:TP, (g % 2) * 8 + k, D:2 * D],
                               start=(g == 0 and k == 0), stop=(g == H - 1 and k == 7))
                last.then_inc(group_used, 1)

            pe.wait_ge(wq_loaded, 48)
            pe.wait_ge(x1_done, NT)
            pe.nop().then_inc(group_used, 2)
            pe.nop().then_inc(y_left, 1)
            queries(0, 0)
            for h in range(H):
                scores(0, h)

            def ffn_tile(t, par, more):
                if more:
                    queries(t + 1, 1 - par)
                for g in range(H):
                    if more and g < 4:
                        scores(t + 1, 2 * g)
                        scores(t + 1, 2 * g + 1)
                    weigh(t, g)

            with pe.Fori(0, NT // 2 - 1) as it:
                ffn_tile(it * 2, 0, True)
                ffn_tile(it * 2 + 1, 1, True)
            ffn_tile(NT - 2, 0, True)
            ffn_tile(NT - 1, 1, False)

        @block.scalar
        def _(act):
            act.nop().then_inc(ct_free, 2)
            with act.Fori(0, NT // 2) as jj:
                for par in range(2):
                    j = jj * 2 + par
                    after(act, ct_full, j + 1)
                    for b in range(3):
                        i0, ni = 4 * b, min(4, NT - 4 * b)
                        last = nc.scalar.activation(
                            CT[0:TP, i0:i0 + ni, bass.ds(j * TP, TP)],
                            ps[0:TP, 3 * par + b, 0:ni * TP].rearrange("p (i d) -> p i d", i=ni), ACT.Copy)
                    last.then_inc(ct_free, 1)
            act.wait_ge(stats_ready, 1)
            nc.scalar.activation(rstd[0:TP, 1, :], rstd[0:TP, 0, :], ACT.Sqrt).then_inc(std_ready, 1)
            act.wait_ge(deg_full, 1)
            for n, (c0, w) in enumerate(COLS):
                last = nc.scalar.activation(dinv_bc[:, c0:c0 + w], ps[:, n, 0:w], ACT.Sqrt)
            for n, (c0, w) in enumerate(COLS):
                last = nc.scalar.activation(deg_bc[:, c0:c0 + w], ps[:, n, 0:w], ACT.Copy)
            last.then_inc(deg_sqrt, 1)
            for t in range(NT):
                act.wait_ge(xnT_full, t + 1)
                nc.scalar.activation(xT[:, :, t * TP:(t + 1) * TP],
                                     ps[:, 4 + t % 4, 0:KC * TP].rearrange("p (c d) -> p c d", c=KC),
                                     ACT.Copy).then_inc(xnT_done, 1)
            for t in range(NT):
                act.wait_ge(kv_full, t + 1)
                if t >= 2:
                    act.wait_ge(kvmm_done, t - 1)
                nc.scalar.activation(k_sb[0:TP, t % 2, :], ps[0:TP, t % 2, :], ACT.Relu).then_inc(k_done, 1)
            for i, (c, n) in enumerate(CHUNKS):
                c0, w = COLS[n]
                act.wait_ge(q_full, i + 1)
                nc.scalar.activation(qT[:, c, c0:c0 + w], ps[:, i % 4, 0:w], ACT.Relu).then_inc(q_done, 1)
            act.wait_ge(dinv_ready, 1)
            act.wait_ge(vec_loaded, 48)

            def layer_h(l):
                for t in range(NT):
                    act.wait_ge(h_full, l * NT + t + 1)
                    nc.scalar.activation(hP[0:TP, t, :], ps[0:TP, t % 4, :], ACT.Copy,
                                         scale=dinv_col[0:TP, t:t + 1]).then_inc(h_done, 1)

            with act.Fori(0, L - 1) as l:
                layer_h(l)
                for i, (c, n) in enumerate(CHUNKS):
                    after(act, z_ready, l * len(CHUNKS) + i + 1)
                    w = COLS[n][1]
                    nc.scalar.activation(z_sb[:, i % 2, 0:w], z_sb[:, i % 2, 0:w], ACT.Identity,
                                         bias=b_col[:, bass.ds(l, 1), c].rearrange("p a -> p a")).then_inc(zb_ready, 1)
            layer_h(L - 1)

            def prepare(t, par):
                act.wait_ge(f_mv, t + 1)
                nc.scalar.activation(fstats[0:TP, 9:10], fstats[0:TP, 8:9], ACT.Sqrt).then_inc(f_std, 1)
                act.wait_ge(xlT_full, t + 1)
                nc.scalar.activation(xlT[:, :, 0:TP], ps[:, 4, 0:KC * TP].rearrange("p (c d) -> p c d", c=KC),
                                     ACT.Copy).then_inc(xlT_done, 1)
                for half in range(2):
                    act.wait_ge(qh_full, t * 2 + half + 1)
                    for hh in range(4):
                        h = 4 * half + hh
                        last = nc.scalar.activation(qh[:, h, 0:TP], ps[:, 5 + half, hh * TP:(hh + 1) * TP],
                                                    ACT.Identity, bias=bq_col[:, h:h + 1])
                    last.then_inc(qh_done, 1)

            def softmax_exp(t):
                act.wait_ge(shift_ready, t + 1)
                nc.scalar.activation(e8[0:TP], e8[0:TP], ACT.Exp).then_inc(exp_done, 1)

            def diagonals(t, g):
                act.wait_ge(vals_ready, t * H + g + 1)
                act.wait_ge(group_used, t * H + g + 1)
                for k in range(8):
                    last = nc.scalar.activation(diag[0:TP, g % 2, k, :], ident[0:TP, 0:TP], ACT.Copy,
                                                scale=vals[0:TP, g, k:k + 1])
                last.then_inc(diag_ready, 1)

            act.wait_ge(wq_loaded, 48)
            prepare(0, 0)
            softmax_exp(0)

            def ffn_tile(t, par, more):
                if more:
                    prepare(t + 1, 1 - par)
                for g in range(H):
                    diagonals(t, g)
                    if more and g == 3:
                        softmax_exp(t + 1)

            with act.Fori(0, NT // 2 - 1) as it:
                ffn_tile(it * 2, 0, True)
                ffn_tile(it * 2 + 1, 1, True)
            ffn_tile(NT - 2, 0, True)
            ffn_tile(NT - 1, 1, False)

        @block.vector
        def _(dve):
            v = nc.vector
            steps = [0]

            def link(ins):
                steps[0] += 1
                ins.then_inc(dve_step, 1)
                dve.wait_ge(dve_step, steps[0])

            dve.wait_ge(iotas_made, 1)
            link(v.tensor_scalar(Eye[:], eye_i[:], 0.0, None, ALU.is_equal))
            v.tensor_scalar(upper[0:NT, 0, :], ahead[0:NT, :], 0.0, None, ALU.is_gt)
            v.tensor_scalar(upper[0:NT, 1, :], ahead[0:NT, :], 0.0, None, ALU.is_ge)
            link(v.tensor_copy(ident[:, 0:TP], Eye[:, 9 * TP:10 * TP]))
            v.nop().then_inc(eye_made, 1)
            dve.wait_ge(edges_loaded, 32)
            link(v.tensor_copy(edge_f[:], edge_i[:]))
            v.nop().then_inc(edges_float, 1)
            v.tensor_reduce(mm[:, 0:1], edge_f[:, 0, :], AX.X, ALU.min)
            link(v.tensor_reduce(mm[:, 1:2], edge_f[:, 0, :], AX.X, ALU.max))
            for k in range(2):
                last = v.tensor_scalar(diag_mm[:, k, :], ident[0:NP, 0:NP], mm[:, k:k + 1], None, ALU.mult)
            last.then_inc(edges_float, 1)
            dve.wait_ge(edges_turned, 1)
            v.tensor_copy(edgeT[0:EB], ps[0:EB, 0, 0:4 * NP].rearrange("p (a b c) -> p a b c", a=2, b=2))
            link(v.tensor_scalar(bnd_hit[0:NT, 0, :], ps[0:NT, 1, 0:NP], thr[0:NT, 1:2], None, ALU.is_le))
            link(v.scalar_tensor_tensor(out=bnd_hit[0:NT, 1, :], in0=ps[0:NT, 1, NP:2 * NP],
                                        scalar=thr[0:NT, 0:1], in1=bnd_hit[0:NT, 0, :],
                                        op0=ALU.is_ge, op1=ALU.mult))
            link(v.tensor_tensor(bnd_hit[0:NT, 0, :], bnd_hit[0:NT, 1, :], iota80[0:NT, 1, :], ALU.mult))
            link(v.tensor_reduce(bnd[0:NT, 0:1], bnd_hit[0:NT, 0, :], AX.X, ALU.max))
            link(v.tensor_tensor(bnd_hit[0:NT, 0, :], bnd_hit[0:NT, 1, :], iota80[0:NT, 0, :], ALU.mult))
            link(v.tensor_reduce(bnd[0:NT, 1:2], bnd_hit[0:NT, 0, :], AX.X, ALU.max))
            link(v.tensor_scalar(bnd[0:NT, 3:4], bnd[0:NT, 0:1], -1.0, float(NP), ALU.mult, ALU.add))
            link(v.tensor_scalar(bnd[0:NT, 0:1], bnd[0:NT, 3:4], float(NP - 1), None, ALU.min))
            link(v.tensor_scalar(bnd[0:NT, 3:4], bnd[0:NT, 0:1], 1.0, None, ALU.add))
            link(v.tensor_tensor(bnd[0:NT, 1:2], bnd[0:NT, 1:2], bnd[0:NT, 3:4], ALU.max))
            link(v.tensor_tensor(bnd[0:NT, 2:3], bnd[0:NT, 1:2], bnd[0:NT, 0:1], ALU.subtract))
            link(v.tensor_scalar(bnd[0:NT, 3:4], bnd[0:NT, 2:3], -1.0, None, ALU.mult))
            v.nop().then_inc(bnd_ready, 1)
            dve.wait_ge(bnd_rows, 1)
            for k in range(3):
                last = v.tensor_copy(bounds[0:1, k, :], ps[0:1, 2 + k, 0:NT])
            link(last)
            v.nop().then_inc(bounds_ready, 1)
            with dve.Fori(0, NT) as j:
                first = dve.value_load(bounds[0:1, 0, bass.ds(j, 1)], min_val=0, max_val=NT * NP - 1)
                end = dve.value_load(bounds[0:1, 1, bass.ds(j, 1)], min_val=1, max_val=NT * NP)
                shift = dve.value_load(bounds[0:1, 2, bass.ds(j, 1)], min_val=-NT * NP, max_val=NP)
                with dve.Fori(first, end) as step:
                    p = nc.s_assert_within(step + shift, 0, NP - 1)
                    for half in range(2):
                        dve.wait_ge(oh_free[half], step + 1)
                        v.tensor_scalar(oh_src[0:EB, half, :], iota_row[0:EB, :],
                                        edgeT[0:EB, 1, half, bass.ds(p, 1)], None, ALU.is_equal)
                        v.tensor_scalar(oh_dst[0:EB, half, 0:TP], iota_row[0:EB, bass.ds(j * TP, TP)],
                                        edgeT[0:EB, 0, half, bass.ds(p, 1)], None, ALU.is_equal
                                        ).then_inc(oh_ready[half], 1)

            dve.wait_ge(x_loaded, 16)
            for t in range(NT):
                last = v.bn_stats(stats[0:TP, t, :], x1[0:TP, t, :])
            link(last)
            for t in range(NT):
                last = v.bn_aggr(mv[0:TP, t, :], stats[0:TP, t, :])
            link(last)
            link(v.tensor_scalar(rstd[0:TP, 0, :], mv[0:TP, :, 1], EPS, None, ALU.add))
            v.nop().then_inc(stats_ready, 1)
            dve.wait_ge(std_ready, 1)
            link(v.reciprocal(rstd[0:TP, 0, :], rstd[0:TP, 1, :]))
            for t in range(NT):
                v.tensor_scalar(xn[0:TP, t, :], x1[0:TP, t, :], mv[0:TP, t, 0:1], rstd[0:TP, 0, t:t + 1],
                                ALU.subtract, ALU.mult).then_inc(xn_ready, 1)

            dve.wait_ge(deg_sqrt, 1)
            link(v.reciprocal(dinv_bc[:], dinv_bc[:]))
            link(v.tensor_tensor(newton[:], dinv_bc[:], dinv_bc[:], ALU.mult))
            link(v.tensor_tensor(newton[:], newton[:], deg_bc[:], ALU.mult))
            link(v.tensor_scalar(newton[:], newton[:], -0.5, 1.5, ALU.mult, ALU.add))
            link(v.tensor_tensor(dinv_bc[:], dinv_bc[:], newton[:], ALU.mult))
            for t in range(NT):
                last = v.tensor_tensor_reduce(newton[0:TP, t * TP:(t + 1) * TP], dinv_bc[0:TP, t * TP:(t + 1) * TP],
                                              ident[0:TP, 0:TP], 1.0, 0.0, ALU.mult, ALU.add,
                                              dinv_col[0:TP, t:t + 1])
            last.then_inc(dinv_ready, 1)

            dve.wait_ge(vones_ready, 1)
            for t in range(NT):
                dve.wait_ge(kv_full, t + 1)
                if t >= 2:
                    dve.wait_ge(kvmm_done, t - 1)
                v.tensor_copy(v_sb[0:TP, t % 2, :, 0:128],
                              ps[0:TP, 2 + t % 2, :].rearrange("p (c d) -> p c d", c=KC)).then_inc(v_done, 1)
            dve.wait_ge(kvmm_done, NT)
            dve.wait_ge(bd_zero, 1)
            dve.wait_ge(vec_loaded, 48)
            for c in range(KC):
                for half in range(2):
                    a = slice(64 * half, 64 * half + 64)
                    v.tensor_scalar(attnBD[a, c, a], ps[a, 4 + c, a], temp_col[a, c:c + 1], None, ALU.mult)
                    last = v.tensor_scalar(ksumBD[a, c, a], ones[a, 0:64], ps[a, 4 + c, 128:129], None, ALU.mult)
            last.then_inc(bd_ready, 1)
            for i, (c, n) in enumerate(CHUNKS):
                c0, w = COLS[n]
                dve.wait_ge(o_full, i + 1)
                link(v.tensor_scalar(newton[:, 0:w], ps[:, 6 + i % 2, 0:w], DEN_MIN, None, ALU.max))
                link(v.reciprocal(newton[:, 512:512 + w], newton[:, 0:w]))
                v.tensor_tensor(outT[:, c, c0:c0 + w], ps[:, 4 + i % 2, 0:w], newton[:, 512:512 + w], ALU.mult
                                ).then_inc(o_done, 1)
            dve.wait_ge(rows_loaded, 32)
            for t in range(NT):
                dve.wait_ge(y_full, t + 1)
                link(v.tensor_tensor(x1[0:TP, t, :], x1[0:TP, t, :], ps[0:TP, t % 4, :], ALU.add))
                v.tensor_tensor(x1[0:TP, t, :], x1[0:TP, t, :], bproj_row[0:TP, :], ALU.add).then_inc(y_done, 1)

            with dve.Fori(0, L - 1) as l:
                for i, (c, n) in enumerate(CHUNKS):
                    c0, w = COLS[n]
                    dve.wait_ge(agg_full, l * len(CHUNKS) + i + 1)
                    v.tensor_tensor(z_sb[:, i % 2, 0:w], ps[:, 4 + i % 4, 0:w], dinv_bc[:, c0:c0 + w], ALU.mult
                                    ).then_inc(z_ready, 1)
                    dve.wait_ge(zb_ready, l * len(CHUNKS) + i + 1)
                    v.scalar_tensor_tensor(out=xT[:, c, c0:c0 + w], in0=z_sb[:, i % 2, 0:w], scalar=SLOPE,
                                           in1=z_sb[:, i % 2, 0:w], op0=ALU.mult, op1=ALU.max
                                           ).then_inc(xt_done, 1)
            for t in range(NT):
                zt = z_sb[0:TP, t % 2, :]
                dve.wait_ge(last_full, t + 1)
                if t >= 2:
                    dve.wait_ge(x1_done, t - 1)
                link(v.scalar_tensor_tensor(out=zt, in0=ps[0:TP, 4 + t % 4, :], scalar=dinv_col[0:TP, t:t + 1],
                                            in1=b_row[0:TP, :], op0=ALU.mult, op1=ALU.add))
                link(v.scalar_tensor_tensor(out=zt, in0=zt, scalar=SLOPE, in1=zt, op0=ALU.mult, op1=ALU.max))
                v.tensor_tensor(x1[0:TP, t, :], x1[0:TP, t, :], zt, ALU.add).then_inc(x1_done, 1)
            dve.wait_ge(x1_done, NT)

            STEPS = 32
            count = [steps[0]]

            def flink(ins):
                count[0] = count[0] + 1
                ins.then_inc(dve_step, 1)
                after(dve, dve_step, count[0])

            def tile_of_x(t):
                return x1[0:TP, t, :] if isinstance(t, int) else \
                    x1[0:TP, bass.ds(t, 1), :].rearrange("p a d -> p (a d)")

            def norm(t, par):
                xt = tile_of_x(t)
                flink(v.bn_stats(fstats[0:TP, 0:6], xt))
                flink(v.bn_aggr(fstats[0:TP, 6:8], fstats[0:TP, 0:6]))
                v.tensor_scalar(fstats[0:TP, 8:9], fstats[0:TP, 7:8], EPS, None, ALU.add).then_inc(f_mv, 1)
                dve.wait_ge(f_std, t + 1)
                flink(v.reciprocal(fstats[0:TP, 10:11], fstats[0:TP, 9:10]))
                v.tensor_scalar(xl[0:TP, par, :], xt, fstats[0:TP, 6:7], fstats[0:TP, 10:11],
                                ALU.subtract, ALU.mult).then_inc(xl_done, 1)

            def top_keys(t, h):
                after(dve, s_full, t * H + h + 1)
                for half in range(2):
                    last = v.max(v8[0:TP, 2 * h + half, :], ps[0:TP, 2 * (h % 2) + half, 0:NK])
                flink(last)
                for half in range(2):
                    last = v.max_index(i8[0:TP, 2 * h + half, :], v8[0:TP, 2 * h + half, :],
                                       ps[0:TP, 2 * (h % 2) + half, 0:NK])
                last.then_inc(s_done, 1)

            def choose(t, par):
                after(dve, s_done, t * H + H)
                halves = v8[0:TP].rearrange("p (h a) k -> p h a k", a=2)
                s4 = sums[0:TP].rearrange("p h (a b) -> p h a b", a=8)
                flink(v.tensor_tensor(s4, halves[:, :, 0, :].unsqueeze(3).to_broadcast([TP, H, 8, 8]),
                                      halves[:, :, 1, :].unsqueeze(2).to_broadcast([TP, H, 8, 8]), ALU.add))
                for h in range(H):
                    last = v.max(best8[0:TP, h, :], sums[0:TP, h, :])
                flink(last)
                for h in range(H):
                    last = v.max_index(pos8[0:TP, h, :], best8[0:TP, h, :], sums[0:TP, h, :])
                flink(last)
                v.tensor_tensor(e8[0:TP], best8[0:TP], best8[0:TP, :, 0:1].to_broadcast([TP, H, 8]),
                                ALU.subtract).then_inc(shift_ready, 1)
                p_flat = pos8[0:TP].rearrange("p h k -> p (h k)")
                v.tensor_scalar(pos_ab[0:TP, 0, :], p_flat, 3, None, ALU.logical_shift_right)
                flink(v.tensor_scalar(pos_ab[0:TP, 1, :], p_flat, 7, None, ALU.bitwise_and))
                indices = i8[0:TP].rearrange("p (h a) k -> p h a k", a=2)
                for ab in range(2):
                    flink(v.tensor_tensor(pick[0:TP], pos_ab[0:TP, ab, :].unsqueeze(2).to_broadcast([TP, 64, 8]),
                                          iota8[0:TP].unsqueeze(1).to_broadcast([TP, 64, 8]), ALU.is_equal))
                    p4 = pick[0:TP].rearrange("p (h k) j -> p h k j", h=H)
                    flink(v.tensor_tensor(p4, p4, indices[:, :, ab, :].unsqueeze(2).to_broadcast([TP, H, 8, 8]),
                                          ALU.mult))
                    flink(v.tensor_reduce(g12[0:TP, ab, :], pick[0:TP], AX.X, ALU.add))
                v.scalar_tensor_tensor(out=idx[0:TP, par, :], in0=g12[0:TP, 0, :], scalar=float(NK),
                                       in1=g12[0:TP, 1, :], op0=ALU.mult, op1=ALU.add).then_inc(idx_ready, 1)
                dve.wait_ge(exp_done, t + 1)
                flink(v.tensor_reduce(esum[0:TP, 0, :], e8[0:TP], AX.X, ALU.add))
                flink(v.reciprocal(esum[0:TP, 1, :], esum[0:TP, 0, :]))
                flink(v.tensor_tensor(p8[0:TP, par], e8[0:TP],
                                      esum[0:TP, 1, :].unsqueeze(2).to_broadcast([TP, H, 8]), ALU.mult))

            def dots(t, par, g):
                for k in range(8):
                    slot = (g % 2) * 8 + k
                    dve.wait_ge(gathered[slot], (t * 4 + g // 2 + 1) * 16)
                    last = v.tensor_tensor_reduce(ring[0:TP, slot, 0:D], ring[0:TP, slot, 0:D], xl[0:TP, par, :],
                                                  1.0, 0.0, ALU.mult, ALU.add, inner[0:TP, g, k:k + 1])
                flink(last)
                v.scalar_tensor_tensor(out=vals[0:TP, g, :], in0=inner[0:TP, g, :], scalar=0.0,
                                       in1=p8[0:TP, par, g, :], op0=ALU.max, op1=ALU.mult
                                       ).then_inc(vals_ready, 1)

            def finish(t, par):
                dve.wait_ge(y_free, t + 1)
                after(dve, group_used, t * H + H + 2)
                v.tensor_tensor(y_sb[0:TP, par, :], ps[0:TP, 7, :], tile_of_x(t), ALU.add).then_inc(y_left, 1)

            def lookup(t, par):
                norm(t, par)
                for h in range(H):
                    top_keys(t, h)
                choose(t, par)

            def ffn_tile(t, par, more):
                if more:
                    norm(t + 1, 1 - par)
                for g in range(H):
                    dots(t, par, g)
                    if more and g < 4:
                        top_keys(t + 1, 2 * g)
                        top_keys(t + 1, 2 * g + 1)
                    if more and g == 4:
                        choose(t + 1, 1 - par)
                finish(t, par)

            dve.wait_ge(idx_zero, 1)
            dve.wait_ge(wq_loaded, 48)
            lookup(0, 0)
            in_loop = count[0]
            with dve.Fori(0, NT // 2 - 1) as it:
                count[0] = it * (2 * STEPS) + in_loop
                ffn_tile(it * 2, 0, True)
                ffn_tile(it * 2 + 1, 1, True)
            count[0] = in_loop + 2 * STEPS * (NT // 2 - 1)
            ffn_tile(NT - 2, 0, True)
            ffn_tile(NT - 1, 1, False)
            assert count[0] == in_loop + STEPS * (NT - 1) + H


def kernel(x, src, dst, L0_gnn_Ws, L0_gnn_bs, L0_mix_Wqkv, L0_mix_temperature, L0_mix_Wproj, L0_mix_bproj,
           L0_ffn_Wq, L0_ffn_bq, L0_ffn_keys, L0_ffn_w_down, L0_ffn_w_up):
    import concourse.bacc as bacc
    from concourse.bass_utils import run_bass_kernel_spmd

    keys = np.asarray(L0_ffn_keys)
    arrays = {
        "x": x, "src": src, "dst": dst, "Ws": L0_gnn_Ws, "bs": L0_gnn_bs,
        "WqkvT": np.asarray(L0_mix_Wqkv).T, "temperature": L0_mix_temperature,
        "WprojT": np.asarray(L0_mix_Wproj).T, "bproj": L0_mix_bproj, "Wq": L0_ffn_Wq, "bq": L0_ffn_bq,
        "keysT": keys.transpose(1, 3, 0, 2).reshape(128, -1),
        "table": np.concatenate([np.asarray(L0_ffn_w_down), np.asarray(L0_ffn_w_up)], axis=1),
    }
    nc = bacc.Bacc("TRN2", target_bir_lowering=False, num_devices=1)
    ins, aps = {}, []
    for name, a in arrays.items():
        ins[f"in_{name}"] = a = np.ascontiguousarray(a)
        aps.append(nc.dram_tensor(f"in_{name}", a.shape, mybir.dt.from_np(a.dtype), kind="ExternalInput").ap())
    out = nc.dram_tensor("out", (N, D), F32, kind="ExternalOutput").ap()
    gps_block(nc, *aps, out)
    r = run_bass_kernel_spmd(nc, [ins], core_ids=[0])
    return r.results[0]["out"]
```

```python
import numpy as np
from contextlib import ExitStack

import concourse.bass as bass
from concourse import mybir

ALU = mybir.AluOpType
ACT = mybir.ActivationFunctionType
AX = mybir.AxisListType
F32 = mybir.dt.float32
F16 = mybir.dt.float16
F32R = mybir.dt.float32r
I32 = mybir.dt.int32
U32 = mybir.dt.uint32

N = 1250
D = 512
E = 20000
TP = 125
NT = N // TP
NC = N + 2
TC = TP + 1
EB = 125
NP = E // (2 * EB)
KC = D // 128
L = 4
H = 8
NK = 256
COLS = [(0, 418), (418, 416), (834, 416)]
SLOPE = 0.01
EPS = 1e-5
DEN_MIN = 100.0
EXACT_DEGREE = 4000.0
QS = 4
QUADS = H * 8 // QS
QSLOTS = 6
CHUNKS = [(c, n) for c in range(KC) for n in range(len(COLS))]


def gps_block(nc, x, src, dst, Ws, bs, WqkvT, temperature, WprojT, bproj, Wq, bq, keysT, table, acc, counts,
              out):
    with ExitStack() as ctx:
        base = [16512]

        def region(nbytes):
            o = base[0]
            base[0] += (nbytes + 31) // 32 * 32
            return o

        def carve(start, end, *specs):
            made, o = [], start
            for name, shape, dt in specs:
                made.append(nc.alloc_sbuf_tensor_at(name, shape, dt, offset=o))
                size = int(np.prod(shape[1:])) * (2 if dt == F16 else 4)
                o += (size + 31) // 32 * 32
            assert o <= end, (specs[0][0], o, end)
            return made

        def sem(name):
            return ctx.enter_context(nc.semaphore(name))

        r_ct, r_h, r_xt, r_w, r_mix = region(50016), region(40960), region(2 * KC * NC * 4), region(16384), region(50016)
        r_misc, r_small, r_end = region(5024 + 4096 + 2048), base[0], 229368

        CT, = carve(r_ct, r_h, ("CT", [128, NT, N], F32R))
        CT_raw, = carve(r_mix, r_misc, ("CT_raw", [128, NT, N], F32))
        CT_lo, = carve(r_mix, r_misc, ("CT_lo", [128, NT, N], F32R))
        hP, = carve(r_h, r_xt, ("hP", [128, 2, NT, D], F32R))
        xT, = carve(r_xt, r_w, ("xT", [128, 2, KC, NC], F32R))
        W, = carve(r_w, r_mix, ("W", [128, 2, KC, D], F32R))
        W_raw, = carve(r_w + 8192, r_mix, ("W_raw", [128, KC, D], F32))
        dinv_bc, z_sb, b_row = carve(r_misc, r_small, ("dinv_bc", [128, N], F32), ("z_sb", [128, 2, D], F32),
                                     ("b_row", [128, D], F32))
        dinv_diag, = carve(r_misc + 5024, r_small, ("dinv_diag", [128, N], F32))
        (ident, ones, b_col, temp_col, row_sum, rstd, dinv_col, dcol, iota8, eps_col, flag_f, flag) = carve(
            r_small, r_end, ("ident", [128, 128], F32), ("ones", [128, 128], F32), ("b_col", [128, L, KC], F32),
            ("temp_col", [128, KC], F32), ("row_sum", [128, 3, NT], F32), ("rstd", [128, 2, NT], F32),
            ("dinv_col", [128, NT], F32), ("dcol", [128, 4, NT], F32), ("iota8", [128, 8], F32),
            ("eps_col", [128, 1], F32), ("flag_f", [1, 2], F32), ("flag", [1, 1], I32))

        wkv, wproj = carve(r_mix, r_misc, ("wkv", [128, 2, KC, 2 * D], F32R), ("wproj", [128, 2, KC, D], F32R))
        wkv_raw, = carve(r_mix + 16384, r_misc, ("wkv_raw", [128, KC, 2 * D], F32))
        wproj_raw, = carve(r_mix + 32768 + 8192, r_misc, ("wproj_raw", [128, KC, D], F32))
        wq, = carve(r_h + 24576, r_xt, ("wq", [128, 2, KC, D], F32R))
        wq_raw, = carve(r_h + 24576 + 8192, r_xt, ("wq_raw", [128, KC, D], F32))
        xn, = carve(r_h, r_h + 24576, ("xn", [128, NT, D], F32))
        kv_f, kv_bd, k_sb, v_sb = carve(
            r_h, r_h + 24576, ("kv_f", [128, KC, 130], F32), ("kv_bd", [128, 2, KC, 130], F32R),
            ("k_sb", [128, 2, 2, D], F32R), ("v_sb", [128, 2, 2, KC, 130], F32R))
        _, _, q_sb, o_sb, o_t = carve(
            r_h, r_h + 24576, ("kv_f_", [128, KC, 130], F32), ("kv_bd_", [128, 2, KC, 130], F32R),
            ("q_sb", [128, 2, 2, KC, TC], F32R), ("o_sb", [128, D], F32), ("o_t", [128, 2, 2, KC, TP], F32R))
        bproj_row, den = carve(r_mix + 49152, r_misc, ("den", [128, 2, 2 * KC], F32), ("den_", [128, 8], F32))
        den, bproj_row = bproj_row, b_row

        (iota_row, Eye, oh_src, oh_dst, edge_i, edge_f, edgeT, mm, thr, ahead, upper, bnd, bnd_i, bounds, bnd_hit,
         diag_mm, pair_no, ct_stage) = carve(
            r_xt, r_w, ("iota_row", [128, N], F16), ("Eye", [128, 19 * TP], F16),
            ("oh_src", [128, 4, N], F16), ("oh_dst", [128, 4, 128], F16),
            ("edge_i", [80, 2, 2 * EB], I32), ("edge_f", [80, 2, 2 * EB], F32), ("edgeT", [128, 2, 2, NP], F32),
            ("mm", [80, 2], F32), ("thr", [16, 2], F32), ("ahead", [16, NT], F32), ("upper", [16, 2, NT], F32),
            ("bnd", [16, 6], F32), ("bnd_i", [16, 2], I32), ("bounds", [1, 4, NT], I32),
            ("bnd_hit", [16, 2, NP], F32), ("diag_mm", [80, 2, NP], F32), ("pair_no", [16, 2, NP], F32),
            ("ct_stage", [128, 2, N], F32))
        eye_i, = carve(r_w, r_mix, ("eye_i", [128, 19 * TP], I32))
        one16, = carve(r_w + 12000, r_mix, ("one16", [128, 2], F16))
        x_sq, = carve(r_w + 12288, r_mix, ("x_sq", [128, D], F32))

        x1, fq, keys, acc_sb = carve(
            r_xt, r_mix, ("x1", [128, NT, D], F32), ("fq", [128, KC, 2 * D], F32), ("keys", [128, H, NK], F32),
            ("acc_sb", [128, 2, D], F32))
        (xl, xlT, qh, v8, i8, sums, pick, best8, pos8, pos_ab, g12, e8, p8, inner, vals, idx, bq_col, esum,
         y_sb, fstats) = carve(
            r_h, r_xt, ("xl", [128, 3, D], F32), ("xlT", [128, KC, 128], F32), ("qh", [128, H, 128], F32),
            ("v8", [128, 2 * H, 8], F32), ("i8", [128, 2 * H, 8], U32), ("sums", [128, H, 64], F32),
            ("pick", [128, 64, 8], F32), ("best8", [128, H, 8], F32), ("pos8", [128, H, 8], U32),
            ("pos_ab", [128, 2, 64], U32), ("g12", [128, 2, 64], F32), ("e8", [128, H, 8], F32),
            ("p8", [128, 3, H * 8], F32), ("inner", [128, H * 8], F32), ("vals", [128, H * 8], F32),
            ("idx", [128, 3, H * 8], U32), ("bq_col", [128, H], F32), ("esum", [128, 2, H], F32),
            ("y_sb", [128, 3, D], F32), ("fstats", [128, 16], F32))
        diag, = carve(r_misc, r_small, ("diag", [128, 4, QS, TP], F32))
        ring_a, = carve(r_mix, r_misc, ("ring_a", [128, 12, 2 * D], F32))
        ring_b, = carve(r_ct, r_h, ("ring_b", [128, 12, 2 * D], F32))

        def row(slot):
            return (ring_a if slot < 12 else ring_b)[:, slot % 12, :]

        ps = ctx.enter_context(nc.psum_tensor("ps", [128, 8, 512], F32))

        edges_loaded, x_loaded, vec_loaded = sem("edges_loaded"), sem("x_loaded"), sem("vec_loaded")
        wkv_loaded, wq_loaded, wproj_loaded, w_loaded = (sem("wkv_loaded"), sem("wq_loaded"),
                                                         sem("wproj_loaded"), sem("w_loaded"))
        wkv_split, wq_split, wproj_split = sem("wkv_split"), sem("wq_split"), sem("wproj_split")
        w_hi, w_split = sem("w_hi"), sem("w_split")
        split_hi = sem("split_hi")
        bproj_loaded, brow_loaded = sem("bproj_loaded"), sem("brow_loaded")
        consts_made, eye_made = sem("consts_made"), sem("eye_made")
        dve_step = sem("dve_step")
        act_step = sem("act_step")
        edges_float = sem("edges_float")
        edges_turned = sem("edges_turned")
        bnd_ready, bnd_rows, bounds_ready = sem("bnd_ready"), sem("bnd_rows"), sem("bounds_ready")
        oh_ready, oh_used = sem("oh_ready"), sem("oh_used")
        ct_full, ct_free = sem("ct_full"), sem("ct_free")
        ct_stored = sem("ct_stored")
        ct_slot_free = sem("ct_slot_free")
        ct_back = sem("ct_back")
        std_ready, rstd_ready, xn_ready = sem("std_ready"), sem("rstd_ready"), sem("xn_ready")
        xnT_full, xnT_hi, xnT_done, pad_zero = sem("xnT_full"), sem("xnT_hi"), sem("xnT_done"), sem("pad_zero")
        ddiag_ready, dinv_full, dinv_ready = sem("ddiag_ready"), sem("dinv_full"), sem("dinv_ready")
        flag_ready, ct_parted = sem("flag_ready"), sem("ct_parted")
        kv_full, kv_hi, kv_done, kvmm_done = sem("kv_full"), sem("kv_hi"), sem("kv_done"), sem("kvmm_done")
        vones_ready, bd_ready = sem("vones_ready"), sem("bd_ready")
        q_full, q_hi, q_done = sem("q_full"), sem("q_hi"), sem("q_done")
        o_full, o_done, ot_full, ot_hi, ot_done = (sem("o_full"), sem("o_done"), sem("ot_full"),
                                                   sem("ot_hi"), sem("ot_done"))
        y_full, y_done, xr_loaded, acc_stored = (sem("y_full"), sem("y_done"),
                                                 [sem(f"xr_loaded{i}") for i in range(2)],
                                                 [sem(f"acc_stored{i}") for i in range(2)])
        h_full, h_hi, h_done = sem("h_full"), sem("h_hi"), sem("h_done")
        agg_full, z_ready, zb_ready, leaky_ready, xt_hi, xt_done = (
            sem("agg_full"), sem("z_ready"), sem("zb_ready"), sem("leaky_ready"), sem("xt_hi"), sem("xt_done"))
        last_full, x1_done = sem("last_full"), sem("x1_done")
        acc_loaded = [sem(f"acc_loaded{i}") for i in range(2)]
        ffn_loaded = sem("ffn_loaded")
        f_mv, f_std, xl_done = sem("f_mv"), sem("f_std"), sem("xl_done")
        xlT_full, xlT_done, qh_full, qh_done = sem("xlT_full"), sem("xlT_done"), sem("qh_full"), sem("qh_done")
        s_full, s_done, shift_ready, exp_done = sem("s_full"), sem("s_done"), sem("shift_ready"), sem("exp_done")
        idx_ready, idx_zero = sem("idx_ready"), sem("idx_zero")
        gathered = [sem(f"gathered{i}") for i in range(QS * QSLOTS)]
        vals_ready, diag_ready = sem("vals_ready"), sem("diag_ready")
        quad_used = sem("quad_used")
        y_left = sem("y_left")
        y_free = sem("y_free")
        out_stored = sem("out_stored")
        waited = sem("waited")

        block = ctx.enter_context(nc.Block())

        def after(engine, signal, value):
            engine.wait_ge(signal, value)
            engine.nop().then_inc(waited, 1)

        def weights(w):
            return w.rearrange("(c p) n -> p c n", p=128)

        @block.sync
        def _(sp):
            sp.dma_start(edge_i[:, 0, :], dst.rearrange("(p e) -> p e", e=2 * EB)).then_inc(edges_loaded, 16)
            sp.dma_start(edge_i[:, 1, :], src.rearrange("(p e) -> p e", e=2 * EB)).then_inc(edges_loaded, 16)
            sp.dma_start(xn[0:TP], x.rearrange("(t p) d -> p t d", p=TP)).then_inc(x_loaded, 16)
            sp.dma_start(wkv_raw[:], weights(WqkvT)[:, :, D:3 * D]).then_inc(wkv_loaded, 16)
            sp.dma_start(wq_raw[:], weights(WqkvT)[:, :, 0:D]).then_inc(wq_loaded, 16)
            sp.dma_start(wproj_raw[:], weights(WprojT)).then_inc(wproj_loaded, 16)
            with nc.allow_non_contiguous_dma("small vectors"):
                sp.dma_start(b_col[:], bs.rearrange("l (c p) -> p l c", p=128)).then_inc(vec_loaded, 16)
                for half in range(2):
                    t_half = temperature.rearrange("(c a) u v -> a (u v) c", a=2)[half]
                    sp.dma_start(temp_col[64 * half:64 * half + 64, :],
                                 t_half.to_broadcast([64, KC])).then_inc(vec_loaded, 16)
            sp.nop().then_inc(ct_slot_free, 2)
            with sp.Fori(0, NT // 2) as jj:
                for par in range(2):
                    j = jj * 2 + par
                    sp.wait_ge(ct_free, j + 3)
                    sp.dma_start(counts[bass.ds(j, 1)].rearrange("a p n -> p (a n)"), ct_stage[0:TP, par, :]
                                 ).then_inc(ct_stored, 16)
                    sp.wait_ge(ct_stored, (j + 1) * 16)
                    sp.nop().then_inc(ct_slot_free, 1)
            sp.dma_start(W_raw[:], weights(Ws[0])).then_inc(w_loaded, 16)
            sp.wait_ge(dinv_full, 1)
            sp.dma_start(bproj_row[0:TP], bproj.rearrange("(a d) -> a d", a=1).to_broadcast([TP, D])
                         ).then_inc(bproj_loaded, 16)
            x_t, acc_t = x.rearrange("(t p) d -> t p d", p=TP), acc.rearrange("(t p) d -> t p d", p=TP)
            for t in range(2):
                sp.dma_start(z_sb[0:TP, t, :], x_t[t]).then_inc(xr_loaded[t], 16)
            for t in range(NT):
                sp.wait_ge(y_done, t + 1)
                sp.dma_start(acc_t[t], z_sb[0:TP, t % 2, :]).then_inc(acc_stored[t % 2], 16)
                sp.wait_ge(acc_stored[t % 2], 16 * (t // 2 + 1))
                if t + 2 < NT:
                    sp.dma_start(z_sb[0:TP, t % 2, :], x_t[t + 2]).then_inc(xr_loaded[t % 2], 16)
            sp.dma_start(b_row[0:TP], bs[L - 1:L, :].to_broadcast([TP, D])).then_inc(brow_loaded, 16)
            for j in range(NT):
                sp.dma_start(CT_raw[0:TP, :, j * TP:(j + 1) * TP], counts[j].rearrange("p (i d) -> p i d", i=NT)
                             ).then_inc(ct_back, 16)
            for l in range(L - 1):
                sp.wait_ge(h_full, NT * (l + 1))
                sp.dma_start(W_raw[:], weights(Ws[l + 1])).then_inc(w_loaded, 16)
            sp.wait_ge(h_full, NT * L)
            for t in range(2):
                sp.dma_start(acc_sb[0:TP, t, :], acc_t[t]).then_inc(acc_loaded[t], 16)
            sp.dma_start(fq[:], weights(Wq)).then_inc(ffn_loaded, 16)
            sp.dma_start(keys[:], keysT.rearrange("p (h n) -> p h n", h=H)).then_inc(ffn_loaded, 16)
            for t in range(2, NT):
                sp.wait_ge(x1_done, t - 1)
                sp.dma_start(acc_sb[0:TP, t % 2, :], acc_t[t]).then_inc(acc_loaded[t % 2], 16)
            sp.wait_ge(last_full, NT)
            with nc.allow_non_contiguous_dma("small vector"):
                sp.dma_start(bq_col[:], bq.rearrange("(h p) -> p h", p=128)).then_inc(ffn_loaded, 16)
            sp.nop().then_inc(y_free, 3)

            def store(it, q):
                t = it * 3 + q
                sp.wait_ge(y_left, t + 2)
                rows = out[t * TP:(t + 1) * TP, :] if isinstance(it, int) else \
                    out[bass.ds(it * (3 * TP) + q * TP, TP), :]
                sp.dma_start(rows, y_sb[0:TP, q]).then_inc(out_stored, 16)
                sp.wait_ge(out_stored, (t + 1) * 16)
                sp.nop().then_inc(y_free, 1)

            with sp.Fori(0, NT // 3) as it:
                for q in range(3):
                    store(it, q)
            store(NT // 3, 0)

        @block.gpsimd
        def _(pool):
            def iota(out_ap, pattern, base_, mult):
                nc.gpsimd.iota(out_ap, pattern, base=base_, channel_multiplier=mult,
                               allow_small_or_imprecise_dtypes=True)

            iota(eye_i[:], [[1, 19 * TP]], -9 * TP, -1)
            iota(ahead[0:NT, :], [[1, NT]], 0, -1)
            iota(thr[0:NT, 0:1], [[0, 1]], 0, TP)
            iota(thr[0:NT, 1:2], [[0, 1]], TP - 1, TP)
            iota(pair_no[0:NT, 0, :], [[1, NP]], 1, 0)
            iota(pair_no[0:NT, 1, :], [[-1, NP]], NP, 0)
            iota(iota_row[:], [[1, N]], 0, 0)
            iota(iota8[:], [[1, 8]], 0, 0)
            nc.gpsimd.memset(one16[:], 1.0)
            nc.gpsimd.memset(eps_col[:], EPS)
            nc.gpsimd.memset(ones[:], 1.0).then_inc(consts_made, 1)

            n_split = 0
            for loaded, w, raw, done in ((wkv_loaded, wkv, wkv_raw, wkv_split), (wq_loaded, wq, wq_raw, wq_split),
                                         (wproj_loaded, wproj, wproj_raw, wproj_split)):
                pool.wait_ge(loaded, 16)
                for c in range(KC):
                    n_split += 1
                    nc.gpsimd.tensor_copy(w[:, 0, c, :], raw[:, c, :]).then_inc(split_hi, 1)
                    pool.wait_ge(split_hi, n_split)
                    last = nc.gpsimd.tensor_tensor(w[:, 1, c, :], raw[:, c, :], w[:, 0, c, :].bitcast(F32),
                                                   ALU.subtract)
                last.then_inc(done, 1)
            pool.wait_ge(ct_full, NT)
            pool.wait_ge(ct_slot_free, NT + 2)
            nc.gpsimd.memset(xT[:, :, :, N:NC].bitcast(F32), 0.0).then_inc(pad_zero, 1)
            pool.wait_ge(xnT_full, NT)
            nc.gpsimd.memset(kv_f[:], 0.0)
            nc.gpsimd.memset(v_sb[:, :, 0].bitcast(F32), 1.0)
            nc.gpsimd.memset(v_sb[:, :, 1].bitcast(F32), 0.0).then_inc(vones_ready, 1)
            pool.wait_ge(last_full, NT)
            nc.gpsimd.memset(idx[:], 0).then_inc(idx_zero, 1)

            def gather_tile(it, q):
                t = it * 3 + q
                pool.wait_ge(idx_ready, t + 1)
                for j in range(QUADS):
                    after(pool, quad_used, t * QUADS + j + 1)
                    for k in range(QS):
                        slot = (q * QUADS + j) % QSLOTS * QS + k
                        nc.gpsimd.indirect_dma_start(
                            out=row(slot), out_offset=None, in_=table,
                            in_offset=bass.IndirectOffsetOnAxis(ap=idx[:, q, QS * j + k:QS * j + k + 1], axis=0),
                        ).then_inc(gathered[slot], 16)

            with pool.Fori(0, NT // 3) as it:
                for q in range(3):
                    gather_tile(it, q)
            gather_tile(NT // 3, 0)

        @block.tensor
        def _(pe):
            mm_ = nc.tensor.matmul

            def split_mm(out_ap, a_hi, a_lo, b_hi, b_lo, start, stop):
                mm_(out_ap, a_hi, b_hi, start=start, stop=False)
                mm_(out_ap, a_hi, b_lo, start=False, stop=False)
                return mm_(out_ap, a_lo, b_hi, start=False, stop=stop)

            pe.wait_ge(eye_made, 1)
            pe.wait_ge(consts_made, 1)
            pe.wait_ge(edges_float, 1)
            for k in range(2):
                for half in range(2):
                    nc.tensor.transpose(ps[0:EB, 0, (2 * k + half) * NP:(2 * k + half + 1) * NP],
                                        edge_f[:, k, half * EB:(half + 1) * EB], ident[0:NP, 0:NP])
            pe.wait_ge(edges_float, 2)
            mm_(ps[0:NT, 1, 0:2 * NP], ones[0:NP, 0:NT], diag_mm[:].rearrange("p a b -> p (a b)"),
                start=True, stop=True).then_inc(edges_turned, 1)
            pe.wait_ge(bnd_ready, 1)
            mm_(ps[0:1, 2, 0:NT], bnd[0:NT, 2:3], upper[0:NT, 0, :], start=True, stop=True)
            mm_(ps[0:1, 3, 0:NT], bnd[0:NT, 2:3], upper[0:NT, 0, :], start=True, stop=False)
            mm_(ps[0:1, 3, 0:NT], bnd[0:NT, 4:5], ident[0:NT, 0:NT], start=False, stop=True)
            mm_(ps[0:1, 4, 0:NT], bnd[0:NT, 2:3], upper[0:NT, 1, :], start=True, stop=True)
            mm_(ps[0:1, 5, 0:NT], bnd[0:NT, 0:1], ident[0:NT, 0:NT], start=True, stop=False)
            mm_(ps[0:1, 5, 0:NT], bnd[0:NT, 3:4], upper[0:NT, 0, :], start=False, stop=True
                ).then_inc(bnd_rows, 1)

            pe.wait_ge(bounds_ready, 1)
            pe.nop().then_inc(oh_used, 4)
            with pe.Fori(0, NT // 2) as jj:
                for par in range(2):
                    j = jj * 2 + par
                    first = pe.value_load(bounds[0:1, 0, bass.ds(j, 1)], min_val=0, max_val=NT * NP - 2)
                    middle = pe.value_load(bounds[0:1, 1, bass.ds(j, 1)], min_val=0, max_val=NT * NP - 1)
                    end = pe.value_load(bounds[0:1, 2, bass.ds(j, 1)], min_val=2, max_val=NT * NP)
                    pe.wait_ge(ct_free, j + 1)
                    mm_(ps[0:TP, 6 + par, 0:1], Eye[0:TP, 9 * TP:10 * TP], one16[0:TP, 0:1],
                        start=True, stop=False, skip_group_check=True)
                    for b in range(3):
                        i0, ni = 4 * b, min(4, NT - 4 * b)
                        mm_(ps[0:TP, 3 * par + b, 0:ni * TP], Eye[0:TP, 9 * TP:10 * TP],
                            Eye[0:TP, bass.ds((9 + i0) * TP - j * TP, ni * TP)],
                            start=True, stop=False, skip_group_check=True)

                    def count_block(slot, number):
                        pe.wait_ge(oh_ready, number + 1)
                        mm_(ps[0:TP, 6 + par, 0:1], oh_dst[0:EB, slot, 0:TP], one16[0:EB, 0:1],
                            start=False, stop=False, skip_group_check=True)
                        for i in range(NT):
                            last = mm_(ps[0:TP, 3 * par + i // 4, (i % 4) * TP:(i % 4 + 1) * TP],
                                       oh_src[0:EB, slot, i * TP:(i + 1) * TP], oh_dst[0:EB, slot, 0:TP],
                                       start=False, stop=False, skip_group_check=True)
                        last.then_inc(oh_used, 1)

                    with pe.If(middle - first):
                        for half in range(2):
                            count_block(2 + half, first * 2 + half)
                    with pe.Fori(middle, end, 2) as step:
                        for slot in range(4):
                            count_block(slot, step * 2 + slot)
                    pe.drain().then_inc(ct_full, 1)

            pe.wait_ge(ct_free, NT + 2)
            for t in range(NT):
                pe.wait_ge(xn_ready, t + 1)
                if t >= 4:
                    pe.wait_ge(xnT_done, t - 3)
                for c in range(KC):
                    last = nc.tensor.transpose(ps[:, 4 + t % 4, c * TP:(c + 1) * TP],
                                               xn[0:TP, t, 128 * c:128 * c + 128], ident[0:TP, 0:TP])
                last.then_inc(xnT_full, 1)
            pe.wait_ge(ddiag_ready, 1)
            for n, (c0, w) in enumerate(COLS):
                last = mm_(ps[:, n, 0:w], ones[0:TP, :], dinv_diag[0:TP, c0:c0 + w], start=True, stop=True)
            last.then_inc(dinv_full, 1)

            def kv_project(t):
                if t >= 2:
                    pe.wait_ge(kv_done, t - 1)
                for which in range(2):
                    for c in range(KC):
                        a, b = slice(t * TP, (t + 1) * TP), slice(which * D, (which + 1) * D)
                        last = split_mm(ps[0:TP, 2 * which + t % 2, :], xT[:, 0, c, a], xT[:, 1, c, a],
                                        wkv[:, 0, c, b], wkv[:, 1, c, b], c == 0, c == KC - 1)
                last.then_inc(kv_full, 1)

            def kv_outer(t):
                pe.wait_ge(kv_done, t + 1)
                for c in range(KC):
                    a = slice(128 * c, 128 * c + 128)
                    last = split_mm(ps[:, 4 + c, 0:130], k_sb[0:TP, t % 2, 0, a], k_sb[0:TP, t % 2, 1, a],
                                    v_sb[0:TP, t % 2, 0, c, :], v_sb[0:TP, t % 2, 1, c, :], t == 0, t == NT - 1)
                last.then_inc(kvmm_done, 1)

            pe.wait_ge(wkv_split, 1)
            pe.wait_ge(xnT_done, NT)
            pe.wait_ge(dinv_ready, 1)
            kv_project(0)
            for t in range(1, NT):
                kv_project(t)
                kv_outer(t - 1)
            kv_outer(NT - 1)

            def query(t):
                if t >= 2:
                    pe.wait_ge(q_done, t - 1)
                for m in range(KC):
                    for c in range(KC):
                        a, b = slice(128 * m, 128 * m + 128), slice(t * TP, t * TP + TC)
                        last = split_mm(ps[:, t % 2, m * TC:(m + 1) * TC], wq[:, 0, c, a], wq[:, 1, c, a],
                                        xT[:, 0, c, b], xT[:, 1, c, b], c == 0, c == KC - 1)
                last.then_inc(q_full, 1)

            def attend(t):
                pe.wait_ge(q_done, t + 1)
                if t == 0:
                    pe.wait_ge(bd_ready, 1)
                else:
                    pe.wait_ge(o_done, t)
                for c in range(KC):
                    last = split_mm(ps[0:TP, 2 + c // 2, c % 2 * 130:(c % 2 + 1) * 130],
                                    q_sb[:, t % 2, 0, c, 0:TP], q_sb[:, t % 2, 1, c, 0:TP],
                                    kv_bd[:, 0, c, :], kv_bd[:, 1, c, :], True, True)
                last.then_inc(o_full, 1)

            def turn(t):
                pe.wait_ge(o_done, t + 1)
                if t >= 2:
                    pe.wait_ge(ot_done, t - 1)
                for c in range(KC):
                    last = nc.tensor.transpose(ps[:, 4 + t % 2, c * TP:(c + 1) * TP],
                                               o_sb[0:TP, 128 * c:128 * c + 128], ident[0:TP, 0:TP])
                last.then_inc(ot_full, 1)

            def project(t):
                pe.wait_ge(ot_done, t + 1)
                if t >= 2:
                    pe.wait_ge(y_done, t - 1)
                for c in range(KC):
                    last = split_mm(ps[0:TP, 6 + t % 2, :], o_t[:, t % 2, 0, c, :], o_t[:, t % 2, 1, c, :],
                                    wproj[:, 0, c, :], wproj[:, 1, c, :], c == 0, c == KC - 1)
                last.then_inc(y_full, 1)

            pe.wait_ge(wq_split, 1)
            pe.wait_ge(wproj_split, 1)
            for i in range(NT + 3):
                if i < NT:
                    query(i)
                if 2 <= i < NT + 2:
                    turn(i - 2)
                if 1 <= i < NT + 1:
                    attend(i - 1)
                if i >= 3:
                    project(i - 3)
            pe.wait_ge(y_done, NT)

            great = pe.value_load(flag[0:1, 0:1], min_val=0, max_val=1)

            def layer_h(l):
                pe.wait_ge(w_split, l + 1)
                for t in range(NT):
                    if t >= 4:
                        pe.wait_ge(h_done, l * NT + t - 3)
                    for c in range(KC):
                        a = slice(t * TP, (t + 1) * TP)
                        last = split_mm(ps[0:TP, t % 4, :], xT[:, 0, c, a], xT[:, 1, c, a],
                                        W[:, 0, c, :], W[:, 1, c, :], c == 0, c == KC - 1)
                    last.then_inc(h_full, 1)
                pe.wait_ge(h_done, l * NT + NT)

            def neighbours(out_ap, s, h_cols, dst_cols, h_first, parts):
                h_parts = [hP[0:TP, i, s, h_cols] for i in range(2)]
                products = [(h_parts[0], CT), (h_parts[1], CT)] + [(h_parts[0], CT_lo)] * (parts - 1)
                for n, (h_part, c_array) in enumerate(products):
                    c_part = c_array[0:TP, s, dst_cols]
                    a, b = (h_part, c_part) if h_first else (c_part, h_part)
                    last = mm_(out_ap, a, b, start=(s == 0 and n == 0),
                               stop=(s == NT - 1 and n == len(products) - 1))
                return last

            def sums(l, parts):
                for i, (c, n) in enumerate(CHUNKS):
                    c0, w = COLS[n]
                    if i >= 4:
                        pe.wait_ge(z_ready, l * len(CHUNKS) + i - 3)
                    for s in range(NT):
                        last = neighbours(ps[:, 4 + i % 4, 0:w], s, slice(128 * c, 128 * c + 128),
                                          slice(c0, c0 + w), True, parts)
                    last.then_inc(agg_full, 1)

            def last_sums(parts):
                for t in range(NT):
                    if t >= 4:
                        pe.wait_ge(x1_done, t - 3)
                    for s in range(NT):
                        last = neighbours(ps[0:TP, 4 + t % 4, :], s, slice(0, D), slice(t * TP, (t + 1) * TP),
                                          False, parts)
                    last.then_inc(last_full, 1)

            pe.wait_ge(ct_parted, 1)
            with pe.Fori(0, L - 1) as l:
                layer_h(l)
                with pe.If(great):
                    sums(l, 2)
                with pe.Else():
                    sums(l, 1)
                pe.wait_ge(xt_done, l * len(CHUNKS) + len(CHUNKS))
            layer_h(L - 1)
            with pe.If(great):
                last_sums(2)
            with pe.Else():
                last_sums(1)

            def queries(t, q):
                pe.wait_ge(xl_done, t + 1)
                for c in range(KC):
                    last = nc.tensor.transpose(ps[:, 4, c * TP:(c + 1) * TP], xl[0:TP, q, 128 * c:128 * c + 128],
                                               ident[0:TP, 0:TP])
                last.then_inc(xlT_full, 1)
                pe.wait_ge(xlT_done, t + 1)
                for half in range(2):
                    for hh in range(4):
                        h = 4 * half + hh
                        for c in range(KC):
                            last = mm_(ps[:, 5 + half, hh * TP:(hh + 1) * TP], fq[:, c, 128 * h:128 * h + 128],
                                       xlT[:, c, 0:TP], start=(c == 0), stop=(c == KC - 1))
                    last.then_inc(qh_full, 1)

            def scores(t, h):
                pe.wait_ge(qh_done, t * 2 + h // 4 + 1)
                if h >= 2 or not isinstance(t, int) or t > 0:
                    pe.wait_ge(s_done, t * H + h - 1)
                for half in range(2):
                    last = mm_(ps[0:TP, 2 * (h % 2) + half, 0:NK], qh[64 * half:64 * half + 64, h, 0:TP],
                               keys[64 * half:64 * half + 64, h, :], start=True, stop=True)
                last.then_inc(s_full, 1)

            def weigh(t, q, j):
                if j == 0:
                    pe.wait_ge(y_left, t + 1)
                pe.wait_ge(diag_ready, t * QUADS + j + 1)
                for k in range(QS):
                    slot = (q * QUADS + j) % QSLOTS * QS + k
                    last = mm_(ps[0:TP, 7, :], diag[0:TP, j % 4, k, :], row(slot)[0:TP, D:2 * D],
                               start=(j == 0 and k == 0), stop=(j == QUADS - 1 and k == QS - 1))
                last.then_inc(quad_used, 1)

            pe.wait_ge(ffn_loaded, 48)
            pe.wait_ge(x1_done, NT)
            pe.nop().then_inc(quad_used, QSLOTS)
            pe.nop().then_inc(y_left, 1)
            queries(0, 0)
            for h in range(H):
                scores(0, h)

            def ffn_tile(it, q, more):
                t = it * 3 + q
                if more:
                    queries(t + 1, (q + 1) % 3)
                for j in range(QUADS):
                    if more and j < H:
                        scores(t + 1, j)
                    weigh(t, q, j)

            with pe.Fori(0, NT // 3) as it:
                for q in range(3):
                    ffn_tile(it, q, True)
            ffn_tile(NT // 3, 0, False)

        @block.scalar
        def _(act):
            steps = [0]

            def link(ins):
                steps[0] += 1
                ins.then_inc(act_step, 1)
                act.wait_ge(act_step, steps[0])

            def a_(out_ap, in_ap, func, **kw):
                return nc.scalar.activation(out_ap, in_ap, func, **kw)

            act.wait_ge(consts_made, 1)
            act.wait_ge(x_loaded, 16)
            for t in range(NT):
                last = a_(x_sq[0:TP], xn[0:TP, t, :], ACT.Copy, accum_out=row_sum[0:TP, 0, t:t + 1])
                link(last)
            link(a_(row_sum[0:TP, 1, :], row_sum[0:TP, 0, :], ACT.Copy, scale=-1.0 / D))
            for t in range(NT):
                link(a_(x_sq[0:TP], xn[0:TP, t, :], ACT.Square, bias=row_sum[0:TP, 1, t:t + 1],
                        accum_out=row_sum[0:TP, 2, t:t + 1]))
            a_(rstd[0:TP, 1, :], row_sum[0:TP, 2, :], ACT.Sqrt, scale=1.0 / D, bias=eps_col[0:TP, 0:1]
               ).then_inc(std_ready, 1)
            act.nop().then_inc(ct_free, 2)
            with act.Fori(0, NT // 2) as jj:
                for par in range(2):
                    j = jj * 2 + par
                    after(act, ct_full, j + 1)
                    a_(dcol[0:TP, 0, bass.ds(j, 1)], ps[0:TP, 6 + par, 0:1], ACT.Copy)
                    act.wait_ge(ct_slot_free, j + 1)
                    for b in range(3):
                        i0, ni = 4 * b, min(4, NT - 4 * b)
                        a_(ct_stage[0:TP, par, i0 * TP:(i0 + ni) * TP], ps[0:TP, 3 * par + b, 0:ni * TP], ACT.Copy)
                    for b in range(3):
                        i0, ni = 4 * b, min(4, NT - 4 * b)
                        last = a_(CT[0:TP, i0:i0 + ni, bass.ds(j * TP, TP)],
                                  ps[0:TP, 3 * par + b, 0:ni * TP].rearrange("p (i d) -> p i d", i=ni), ACT.Copy)
                    last.then_inc(ct_free, 1)
            act.wait_ge(ct_free, NT + 2)
            a_(dcol[0:TP, 1, :], dcol[0:TP, 0, :], ACT.Sqrt).then_inc(std_ready, 1)
            act.wait_ge(pad_zero, 1)
            for t in range(NT):
                act.wait_ge(xnT_full, t + 1)
                a_(xT[:, 0, :, t * TP:(t + 1) * TP],
                   ps[:, 4 + t % 4, 0:KC * TP].rearrange("p (c d) -> p c d", c=KC), ACT.Copy).then_inc(xnT_hi, 1)
            act.wait_ge(dinv_full, 1)
            for n, (c0, w) in enumerate(COLS):
                last = a_(dinv_bc[:, c0:c0 + w], ps[:, n, 0:w], ACT.Copy)
            last.then_inc(dinv_ready, 1)
            act.wait_ge(vones_ready, 1)
            for t in range(NT):
                act.wait_ge(kv_full, t + 1)
                if t >= 2:
                    act.wait_ge(kvmm_done, t - 1)
                a_(k_sb[0:TP, t % 2, 0, :], ps[0:TP, t % 2, :], ACT.Relu)
                a_(v_sb[0:TP, t % 2, 0, :, 0:128], ps[0:TP, 2 + t % 2, :].rearrange("p (c d) -> p c d", c=KC),
                   ACT.Copy).then_inc(kv_hi, 1)
            act.wait_ge(w_loaded, 16)
            a_(W[:, 0], W_raw[:], ACT.Copy).then_inc(w_hi, 1)

            def q_high(t):
                act.wait_ge(q_full, t + 1)
                if t == 0:
                    act.wait_ge(kvmm_done, NT)
                if t >= 2:
                    act.wait_ge(o_full, t - 1)
                a_(q_sb[:, t % 2, 0], ps[:, t % 2, 0:KC * TC].rearrange("p (c d) -> p c d", c=KC), ACT.Relu
                   ).then_inc(q_hi, 1)

            def o_high(t):
                act.wait_ge(ot_full, t + 1)
                if t >= 2:
                    act.wait_ge(y_full, t - 1)
                a_(o_t[:, t % 2, 0], ps[:, 4 + t % 2, 0:KC * TP].rearrange("p (c d) -> p c d", c=KC), ACT.Copy
                   ).then_inc(ot_hi, 1)

            for i in range(NT + 2):
                if i < NT:
                    q_high(i)
                if i >= 2:
                    o_high(i - 2)

            act.wait_ge(dinv_ready, 1)
            act.wait_ge(vec_loaded, 48)

            def layer_h(l):
                for t in range(NT):
                    act.wait_ge(h_full, l * NT + t + 1)
                    a_(hP[0:TP, 0, t, :], ps[0:TP, t % 4, :], ACT.Copy, scale=dinv_col[0:TP, t:t + 1]
                       ).then_inc(h_hi, 1)

            def leaky_high(l, i):
                c, n = CHUNKS[i]
                c0, w = COLS[n]
                after(act, leaky_ready, l * len(CHUNKS) + i + 1)
                a_(xT[:, 0, c, c0:c0 + w], z_sb[:, i % 2, 0:w], ACT.Copy).then_inc(xt_hi, 1)

            with act.Fori(0, L - 1) as l:
                layer_h(l)
                after(act, w_loaded, l * 16 + 32)
                a_(W[:, 0], W_raw[:], ACT.Copy).then_inc(w_hi, 1)
                for i, (c, n) in enumerate(CHUNKS):
                    after(act, z_ready, l * len(CHUNKS) + i + 1)
                    w = COLS[n][1]
                    a_(z_sb[:, i % 2, 0:w], z_sb[:, i % 2, 0:w], ACT.Identity,
                       bias=b_col[:, bass.ds(l, 1), c].rearrange("p a -> p a")).then_inc(zb_ready, 1)
                    leaky_high(l, i)
            layer_h(L - 1)

            def prepare(t):
                act.wait_ge(f_mv, t + 1)
                a_(fstats[0:TP, 9:10], fstats[0:TP, 8:9], ACT.Sqrt).then_inc(f_std, 1)
                act.wait_ge(xlT_full, t + 1)
                a_(xlT[:, :, 0:TP], ps[:, 4, 0:KC * TP].rearrange("p (c d) -> p c d", c=KC), ACT.Copy
                   ).then_inc(xlT_done, 1)
                for half in range(2):
                    act.wait_ge(qh_full, t * 2 + half + 1)
                    for hh in range(4):
                        h = 4 * half + hh
                        last = a_(qh[:, h, 0:TP], ps[:, 5 + half, hh * TP:(hh + 1) * TP], ACT.Identity,
                                  bias=bq_col[:, h:h + 1])
                    last.then_inc(qh_done, 1)

            def softmax_exp(t):
                act.wait_ge(shift_ready, t + 1)
                a_(e8[0:TP], e8[0:TP], ACT.Exp).then_inc(exp_done, 1)

            def diagonals(t, j):
                act.wait_ge(vals_ready, t * QUADS + j + 1)
                act.wait_ge(quad_used, t * QUADS + j + QSLOTS - 3)
                for k in range(QS):
                    last = a_(diag[0:TP, j % 4, k, :], ident[0:TP, 0:TP], ACT.Copy,
                              scale=vals[0:TP, QS * j + k:QS * j + k + 1])
                last.then_inc(diag_ready, 1)

            act.wait_ge(ffn_loaded, 48)
            prepare(0)
            softmax_exp(0)

            def ffn_tile(it, q, more):
                t = it * 3 + q
                if more:
                    prepare(t + 1)
                for j in range(QUADS):
                    diagonals(t, j)
                    if more and j == H:
                        softmax_exp(t + 1)

            with act.Fori(0, NT // 3) as it:
                for q in range(3):
                    ffn_tile(it, q, True)
            ffn_tile(NT // 3, 0, False)

        @block.vector
        def _(dve):
            v = nc.vector
            steps = [0]

            def link(ins):
                steps[0] += 1
                ins.then_inc(dve_step, 1)
                dve.wait_ge(dve_step, steps[0])

            def low(out_ap, in_ap, hi_ap, op0=ALU.bypass, scalar=0.0):
                if op0 == ALU.bypass:
                    return v.tensor_tensor(out_ap, in_ap, hi_ap.bitcast(F32), ALU.subtract)
                return v.scalar_tensor_tensor(out=out_ap, in0=in_ap, scalar=scalar, in1=hi_ap.bitcast(F32),
                                              op0=op0, op1=ALU.subtract)

            dve.wait_ge(consts_made, 1)
            link(v.tensor_scalar(Eye[:], eye_i[:], 0.0, None, ALU.is_equal))
            v.tensor_scalar(upper[0:NT, 0, :], ahead[0:NT, :], 0.0, None, ALU.is_gt)
            v.tensor_scalar(upper[0:NT, 1, :], ahead[0:NT, :], 0.0, None, ALU.is_ge)
            link(v.tensor_copy(ident[:, 0:TP], Eye[:, 9 * TP:10 * TP]))
            v.nop().then_inc(eye_made, 1)
            dve.wait_ge(edges_loaded, 32)
            link(v.tensor_copy(edge_f[:], edge_i[:]))
            v.nop().then_inc(edges_float, 1)
            v.tensor_reduce(mm[:, 0:1], edge_f[:, 0, :], AX.X, ALU.min)
            link(v.tensor_reduce(mm[:, 1:2], edge_f[:, 0, :], AX.X, ALU.max))
            for k in range(2):
                last = v.tensor_scalar(diag_mm[:, k, :], ident[0:NP, 0:NP], mm[:, k:k + 1], None, ALU.mult)
            last.then_inc(edges_float, 1)
            dve.wait_ge(edges_turned, 1)
            v.tensor_copy(edgeT[0:EB], ps[0:EB, 0, 0:4 * NP].rearrange("p (a b c) -> p a b c", a=2, b=2))
            B = bnd[0:NT]
            link(v.tensor_scalar(bnd_hit[0:NT, 0, :], ps[0:NT, 1, 0:NP], thr[0:NT, 1:2], None, ALU.is_le))
            link(v.scalar_tensor_tensor(out=bnd_hit[0:NT, 1, :], in0=ps[0:NT, 1, NP:2 * NP],
                                        scalar=thr[0:NT, 0:1], in1=bnd_hit[0:NT, 0, :],
                                        op0=ALU.is_ge, op1=ALU.mult))
            link(v.tensor_tensor(bnd_hit[0:NT, 0, :], bnd_hit[0:NT, 1, :], pair_no[0:NT, 1, :], ALU.mult))
            link(v.tensor_reduce(B[:, 0:1], bnd_hit[0:NT, 0, :], AX.X, ALU.max))
            link(v.tensor_tensor(bnd_hit[0:NT, 0, :], bnd_hit[0:NT, 1, :], pair_no[0:NT, 0, :], ALU.mult))
            link(v.tensor_reduce(B[:, 1:2], bnd_hit[0:NT, 0, :], AX.X, ALU.max))
            link(v.tensor_scalar(B[:, 3:4], B[:, 0:1], -1.0, float(NP), ALU.mult, ALU.add))
            link(v.tensor_scalar(B[:, 0:1], B[:, 3:4], float(NP - 2), None, ALU.min))
            link(v.tensor_scalar(B[:, 3:4], B[:, 0:1], 2.0, None, ALU.add))
            link(v.tensor_tensor(B[:, 1:2], B[:, 1:2], B[:, 3:4], ALU.max))
            link(v.tensor_tensor(B[:, 2:3], B[:, 1:2], B[:, 0:1], ALU.subtract))
            v.tensor_scalar(B[:, 3:4], B[:, 2:3], -1.0, None, ALU.mult)
            link(v.tensor_copy(bnd_i[0:NT, 0:1], B[:, 2:3]))
            link(v.tensor_scalar(bnd_i[0:NT, 1:2], bnd_i[0:NT, 0:1], 1, None, ALU.bitwise_and))
            link(v.tensor_copy(B[:, 4:5], bnd_i[0:NT, 1:2]))
            v.nop().then_inc(bnd_ready, 1)
            dve.wait_ge(bnd_rows, 1)
            for k in range(4):
                last = v.tensor_copy(bounds[0:1, k, :], ps[0:1, 2 + k, 0:NT])
            link(last)
            v.nop().then_inc(bounds_ready, 1)

            with dve.Fori(0, NT) as j:
                first = dve.value_load(bounds[0:1, 0, bass.ds(j, 1)], min_val=0, max_val=NT * NP - 2)
                middle = dve.value_load(bounds[0:1, 1, bass.ds(j, 1)], min_val=0, max_val=NT * NP - 1)
                end = dve.value_load(bounds[0:1, 2, bass.ds(j, 1)], min_val=2, max_val=NT * NP)
                shift = dve.value_load(bounds[0:1, 3, bass.ds(j, 1)], min_val=-NT * NP, max_val=NP)

                def one_hot(slot, pair, half, used):
                    dve.wait_ge(oh_used, used)
                    v.tensor_scalar(oh_src[0:EB, slot, :], iota_row[0:EB, :],
                                    edgeT[0:EB, 1, half, bass.ds(pair, 1)], None, ALU.is_equal)
                    v.tensor_scalar(oh_dst[0:EB, slot, 0:TP], iota_row[0:EB, bass.ds(j * TP, TP)],
                                    edgeT[0:EB, 0, half, bass.ds(pair, 1)], None, ALU.is_equal
                                    ).then_inc(oh_ready, 1)

                with dve.If(middle - first):
                    pair = nc.s_assert_within(first + shift, 0, NP - 1)
                    for half in range(2):
                        one_hot(2 + half, pair, half, first * 2 + half + 3)
                with dve.Fori(middle, end, 2) as step:
                    for slot in range(4):
                        pair = nc.s_assert_within(step + shift + slot // 2, 0, NP - 1)
                        one_hot(slot, pair, slot % 2, step * 2 + slot + 1)

            dve.wait_ge(std_ready, 1)
            link(v.reciprocal(rstd[0:TP, 0, :], rstd[0:TP, 1, :]))
            for t in range(NT):
                v.tensor_scalar(xn[0:TP, t, :], xn[0:TP, t, :], row_sum[0:TP, 1, t:t + 1], rstd[0:TP, 0, t:t + 1],
                                ALU.add, ALU.mult).then_inc(xn_ready, 1)

            dve.wait_ge(std_ready, 2)
            link(v.reciprocal(dcol[0:TP, 1, :], dcol[0:TP, 1, :]))
            link(v.tensor_tensor(dcol[0:TP, 2, :], dcol[0:TP, 1, :], dcol[0:TP, 1, :], ALU.mult))
            link(v.tensor_tensor(dcol[0:TP, 3, :], dcol[0:TP, 2, :], dcol[0:TP, 0, :], ALU.mult))
            link(v.tensor_scalar(dcol[0:TP, 2, :], dcol[0:TP, 3, :], -0.5, 1.5, ALU.mult, ALU.add))
            link(v.tensor_tensor(dinv_col[0:TP], dcol[0:TP, 1, :], dcol[0:TP, 2, :], ALU.mult))
            v.tensor_tensor(dinv_diag[0:TP].rearrange("p (t d) -> p t d", t=NT),
                            ident[0:TP, 0:TP].unsqueeze(1).to_broadcast([TP, NT, TP]),
                            dinv_col[0:TP].unsqueeze(2).to_broadcast([TP, NT, TP]), ALU.mult
                            ).then_inc(ddiag_ready, 1)
            for t in range(NT):
                dve.wait_ge(xnT_hi, t + 1)
                low(xT[:, 1, :, t * TP:(t + 1) * TP],
                    ps[:, 4 + t % 4, 0:KC * TP].rearrange("p (c d) -> p c d", c=KC),
                    xT[:, 0, :, t * TP:(t + 1) * TP]).then_inc(xnT_done, 1)
            dve.wait_ge(dinv_ready, 1)
            link(v.tensor_reduce(flag_f[0:1, 0:1], dinv_bc[0:1, :], AX.X, ALU.min))
            link(v.tensor_scalar(flag_f[0:1, 1:2], flag_f[0:1, 0:1], EXACT_DEGREE ** -0.5, None, ALU.is_lt))
            link(v.tensor_copy(flag[:], flag_f[0:1, 1:2]))

            dve.wait_ge(vones_ready, 1)
            for t in range(NT):
                dve.wait_ge(kv_hi, t + 1)
                low(k_sb[0:TP, t % 2, 1, :], ps[0:TP, t % 2, :], k_sb[0:TP, t % 2, 0, :], ALU.max, 0.0)
                low(v_sb[0:TP, t % 2, 1, :, 0:128], ps[0:TP, 2 + t % 2, :].rearrange("p (c d) -> p c d", c=KC),
                    v_sb[0:TP, t % 2, 0, :, 0:128]).then_inc(kv_done, 1)
            dve.wait_ge(kvmm_done, NT)
            dve.wait_ge(vec_loaded, 48)
            for c in range(KC):
                for half in range(2):
                    a = slice(64 * half, 64 * half + 64)
                    v.tensor_scalar(kv_f[a, c, a], ps[a, 4 + c, a], temp_col[a, c:c + 1], None, ALU.mult)
                    last = v.tensor_copy(kv_f[a, c, 128 + half:129 + half], ps[a, 4 + c, 128:129])
            link(last)
            link(v.tensor_copy(kv_bd[:, 0], kv_f[:]))
            low(kv_bd[:, 1], kv_f[:], kv_bd[:, 0]).then_inc(bd_ready, 1)

            def q_low(t):
                dve.wait_ge(q_hi, t + 1)
                low(q_sb[:, t % 2, 1], ps[:, t % 2, 0:KC * TC].rearrange("p (c d) -> p c d", c=KC),
                    q_sb[:, t % 2, 0], ALU.max, 0.0).then_inc(q_done, 1)

            def divide(t):
                dve.wait_ge(o_full, t + 1)
                if t >= 1:
                    dve.wait_ge(ot_full, t)
                outs = ps[0:TP, 2:4, 0:260].rearrange("p b (c d) -> p b c d", c=2)
                link(v.tensor_scalar(den[0:TP, 0, :].rearrange("p (b c d) -> p b c d", b=2, c=2),
                                     outs[:, :, :, 128:130], DEN_MIN, None, ALU.max))
                link(v.reciprocal(den[0:TP, 1, :], den[0:TP, 0, :]))
                for b in range(2):
                    last = v.tensor_tensor(
                        o_sb[0:TP, 256 * b:256 * b + 256].rearrange("p (c a d) -> p c a d", c=2, a=2),
                        outs[:, b, :, 0:128].rearrange("p c (a d) -> p c a d", a=2),
                        den[0:TP, 1, 4 * b:4 * b + 4].rearrange("p (c a) -> p c a", c=2).unsqueeze(3)
                        .to_broadcast([TP, 2, 2, 64]), ALU.mult)
                last.then_inc(o_done, 1)

            def o_low(t):
                dve.wait_ge(ot_hi, t + 1)
                low(o_t[:, t % 2, 1], ps[:, 4 + t % 2, 0:KC * TP].rearrange("p (c d) -> p c d", c=KC),
                    o_t[:, t % 2, 0]).then_inc(ot_done, 1)

            def residual(t):
                zt = z_sb[0:TP, t % 2, :]
                dve.wait_ge(y_full, t + 1)
                dve.wait_ge(xr_loaded[t % 2], 16 * (t // 2 + 1))
                link(v.tensor_tensor(zt, zt, ps[0:TP, 6 + t % 2, :], ALU.add))
                v.tensor_tensor(zt, zt, bproj_row[0:TP, :], ALU.add).then_inc(y_done, 1)

            dve.wait_ge(bproj_loaded, 16)
            for i in range(NT + 3):
                if i < NT:
                    q_low(i)
                if 2 <= i < NT + 2:
                    o_low(i - 2)
                if 1 <= i < NT + 1:
                    divide(i - 1)
                if i >= 3:
                    residual(i - 3)
                if i == 4:
                    dve.wait_ge(w_hi, 1)
                    low(W[:, 1], W_raw[:], W[:, 0]).then_inc(w_split, 1)

            great = dve.value_load(flag[0:1, 0:1], min_val=0, max_val=1)
            dve.wait_ge(ct_back, 16 * NT)
            with dve.If(great):
                for s in range(NT):
                    low(CT_lo[0:TP, s, :], CT_raw[0:TP, s, :], CT[0:TP, s, :])
                dve.drain()
            v.nop().then_inc(ct_parted, 1)

            def h_low(l):
                for t in range(NT):
                    dve.wait_ge(h_hi, l * NT + t + 1)
                    low(hP[0:TP, 1, t, :], ps[0:TP, t % 4, :], hP[0:TP, 0, t, :], ALU.mult,
                        dinv_col[0:TP, t:t + 1]).then_inc(h_done, 1)

            for buf in range(2):
                dve.wait_ge(acc_stored[buf], 16 * (NT // 2))
            with dve.Fori(0, L - 1) as l:
                h_low(l)
                for i, (c, n) in enumerate(CHUNKS):
                    c0, w = COLS[n]
                    if i >= 2:
                        dve.wait_ge(xt_done, l * len(CHUNKS) + i - 1)
                    dve.wait_ge(agg_full, l * len(CHUNKS) + i + 1)
                    v.tensor_tensor(z_sb[:, i % 2, 0:w], ps[:, 4 + i % 4, 0:w], dinv_bc[:, c0:c0 + w], ALU.mult
                                    ).then_inc(z_ready, 1)
                    if i == 0:
                        dve.wait_ge(w_hi, l + 2)
                        low(W[:, 1], W_raw[:], W[:, 0]).then_inc(w_split, 1)
                    dve.wait_ge(zb_ready, l * len(CHUNKS) + i + 1)
                    v.scalar_tensor_tensor(out=z_sb[:, i % 2, 0:w], in0=z_sb[:, i % 2, 0:w], scalar=SLOPE,
                                           in1=z_sb[:, i % 2, 0:w], op0=ALU.mult, op1=ALU.max
                                           ).then_inc(leaky_ready, 1)
                    dve.wait_ge(xt_hi, l * len(CHUNKS) + i + 1)
                    low(xT[:, 1, c, c0:c0 + w], z_sb[:, i % 2, 0:w], xT[:, 0, c, c0:c0 + w]).then_inc(xt_done, 1)
                dve.wait_ge(xt_done, l * len(CHUNKS) + len(CHUNKS))
            h_low(L - 1)
            dve.wait_ge(brow_loaded, 16)
            for t in range(NT):
                zt = z_sb[0:TP, t % 2, :]
                dve.wait_ge(last_full, t + 1)
                if t >= 2:
                    dve.wait_ge(x1_done, t - 1)
                link(v.scalar_tensor_tensor(out=zt, in0=ps[0:TP, 4 + t % 4, :], scalar=dinv_col[0:TP, t:t + 1],
                                            in1=b_row[0:TP, :], op0=ALU.mult, op1=ALU.add))
                link(v.scalar_tensor_tensor(out=zt, in0=zt, scalar=SLOPE, in1=zt, op0=ALU.mult, op1=ALU.max))
                dve.wait_ge(acc_loaded[t % 2], 16 * (t // 2 + 1))
                v.tensor_tensor(x1[0:TP, t, :], acc_sb[0:TP, t % 2, :], zt, ALU.add).then_inc(x1_done, 1)
            dve.wait_ge(x1_done, NT)

            STEPS = 24 + QUADS
            count = [steps[0]]

            def flink(ins):
                count[0] = count[0] + 1
                ins.then_inc(dve_step, 1)
                after(dve, dve_step, count[0])

            def tile_of_x(t):
                return x1[0:TP, t, :] if isinstance(t, int) else \
                    x1[0:TP, bass.ds(t, 1), :].rearrange("p a d -> p (a d)")

            def norm(t, q):
                xt = tile_of_x(t)
                flink(v.bn_stats(fstats[0:TP, 0:6], xt))
                flink(v.bn_aggr(fstats[0:TP, 6:8], fstats[0:TP, 0:6]))
                v.tensor_scalar(fstats[0:TP, 8:9], fstats[0:TP, 7:8], EPS, None, ALU.add).then_inc(f_mv, 1)
                dve.wait_ge(f_std, t + 1)
                flink(v.reciprocal(fstats[0:TP, 10:11], fstats[0:TP, 9:10]))
                v.tensor_scalar(xl[0:TP, q, :], xt, fstats[0:TP, 6:7], fstats[0:TP, 10:11],
                                ALU.subtract, ALU.mult).then_inc(xl_done, 1)

            def top_keys(t, h):
                after(dve, s_full, t * H + h + 1)
                for half in range(2):
                    last = v.max(v8[0:TP, 2 * h + half, :], ps[0:TP, 2 * (h % 2) + half, 0:NK])
                flink(last)
                for half in range(2):
                    last = v.max_index(i8[0:TP, 2 * h + half, :], v8[0:TP, 2 * h + half, :],
                                       ps[0:TP, 2 * (h % 2) + half, 0:NK])
                last.then_inc(s_done, 1)

            def choose(t):
                after(dve, s_done, t * H + H)
                halves = v8[0:TP].rearrange("p (h a) k -> p h a k", a=2)
                s4 = sums[0:TP].rearrange("p h (a b) -> p h a b", a=8)
                flink(v.tensor_tensor(s4, halves[:, :, 0, :].unsqueeze(3).to_broadcast([TP, H, 8, 8]),
                                      halves[:, :, 1, :].unsqueeze(2).to_broadcast([TP, H, 8, 8]), ALU.add))
                for h in range(H):
                    last = v.max(best8[0:TP, h, :], sums[0:TP, h, :])
                flink(last)
                for h in range(H):
                    last = v.max_index(pos8[0:TP, h, :], best8[0:TP, h, :], sums[0:TP, h, :])
                flink(last)
                v.tensor_tensor(e8[0:TP], best8[0:TP], best8[0:TP, :, 0:1].to_broadcast([TP, H, 8]),
                                ALU.subtract).then_inc(shift_ready, 1)

            def name_rows(t, q):
                p_flat = pos8[0:TP].rearrange("p h k -> p (h k)")
                v.tensor_scalar(pos_ab[0:TP, 0, :], p_flat, 3, None, ALU.logical_shift_right)
                flink(v.tensor_scalar(pos_ab[0:TP, 1, :], p_flat, 7, None, ALU.bitwise_and))
                indices = i8[0:TP].rearrange("p (h a) k -> p h a k", a=2)
                for ab in range(2):
                    flink(v.tensor_tensor(pick[0:TP], pos_ab[0:TP, ab, :].unsqueeze(2).to_broadcast([TP, 64, 8]),
                                          iota8[0:TP].unsqueeze(1).to_broadcast([TP, 64, 8]), ALU.is_equal))
                    p4 = pick[0:TP].rearrange("p (h k) j -> p h k j", h=H)
                    flink(v.tensor_tensor(p4, p4, indices[:, :, ab, :].unsqueeze(2).to_broadcast([TP, H, 8, 8]),
                                          ALU.mult))
                    flink(v.tensor_reduce(g12[0:TP, ab, :], pick[0:TP], AX.X, ALU.add))
                v.scalar_tensor_tensor(out=idx[0:TP, q, :], in0=g12[0:TP, 0, :], scalar=float(NK),
                                       in1=g12[0:TP, 1, :], op0=ALU.mult, op1=ALU.add).then_inc(idx_ready, 1)

            def softmax(t, q):
                dve.wait_ge(exp_done, t + 1)
                flink(v.tensor_reduce(esum[0:TP, 0, :], e8[0:TP], AX.X, ALU.add))
                flink(v.reciprocal(esum[0:TP, 1, :], esum[0:TP, 0, :]))
                flink(v.tensor_tensor(p8[0:TP, q].rearrange("p (h k) -> p h k", h=H), e8[0:TP],
                                      esum[0:TP, 1, :].unsqueeze(2).to_broadcast([TP, H, 8]), ALU.mult))

            def dots(it, q, j):
                n = q * QUADS + j
                for k in range(QS):
                    slot = n % QSLOTS * QS + k
                    dve.wait_ge(gathered[slot], (it * (3 * QUADS // QSLOTS) + n // QSLOTS + 1) * 16)
                    last = v.tensor_tensor_reduce(row(slot)[0:TP, 0:D], row(slot)[0:TP, 0:D], xl[0:TP, q, :],
                                                  1.0, 0.0, ALU.mult, ALU.add,
                                                  inner[0:TP, QS * j + k:QS * j + k + 1])
                flink(last)
                quad = slice(QS * j, QS * j + QS)
                v.scalar_tensor_tensor(out=vals[0:TP, quad], in0=inner[0:TP, quad], scalar=0.0,
                                       in1=p8[0:TP, q, quad], op0=ALU.max, op1=ALU.mult).then_inc(vals_ready, 1)

            def finish(t, q):
                dve.wait_ge(y_free, t + 1)
                after(dve, quad_used, t * QUADS + QUADS + QSLOTS)
                v.tensor_tensor(y_sb[0:TP, q, :], ps[0:TP, 7, :], tile_of_x(t), ALU.add).then_inc(y_left, 1)

            def ffn_tile(it, q, more):
                t, nq = it * 3 + q, (q + 1) % 3
                if more:
                    norm(t + 1, nq)
                for j in range(QUADS):
                    dots(it, q, j)
                    if more and j < H:
                        top_keys(t + 1, j)
                    if more and j == H:
                        choose(t + 1)
                    if more and j == H + 1:
                        name_rows(t + 1, nq)
                    if more and j == H + 2:
                        softmax(t + 1, nq)
                finish(t, q)

            dve.wait_ge(idx_zero, 1)
            dve.wait_ge(ffn_loaded, 48)
            norm(0, 0)
            for h in range(H):
                top_keys(0, h)
            choose(0)
            name_rows(0, 0)
            softmax(0, 0)
            in_loop = count[0]
            with dve.Fori(0, NT // 3) as it:
                count[0] = it * (3 * STEPS) + in_loop
                for q in range(3):
                    ffn_tile(it, q, True)
            count[0] = in_loop + STEPS * (NT - 1)
            ffn_tile(NT // 3, 0, False)


def kernel(x, src, dst, L0_gnn_Ws, L0_gnn_bs, L0_mix_Wqkv, L0_mix_temperature, L0_mix_Wproj, L0_mix_bproj,
           L0_ffn_Wq, L0_ffn_bq, L0_ffn_keys, L0_ffn_w_down, L0_ffn_w_up):
    import concourse.bacc as bacc
    from concourse.bass_utils import run_bass_kernel_spmd

    keys = np.asarray(L0_ffn_keys)
    arrays = {
        "x": x, "src": src, "dst": dst, "Ws": L0_gnn_Ws, "bs": L0_gnn_bs,
        "WqkvT": np.asarray(L0_mix_Wqkv).T, "temperature": L0_mix_temperature,
        "WprojT": np.asarray(L0_mix_Wproj).T, "bproj": L0_mix_bproj, "Wq": L0_ffn_Wq, "bq": L0_ffn_bq,
        "keysT": keys.transpose(1, 3, 0, 2).reshape(128, -1),
        "table": np.concatenate([np.asarray(L0_ffn_w_down), np.asarray(L0_ffn_w_up)], axis=1),
    }
    nc = bacc.Bacc("TRN2", target_bir_lowering=False, num_devices=1)
    ins, aps = {}, []
    for name, a in arrays.items():
        ins[f"in_{name}"] = a = np.ascontiguousarray(a)
        aps.append(nc.dram_tensor(f"in_{name}", a.shape, mybir.dt.from_np(a.dtype), kind="ExternalInput").ap())
    out = nc.dram_tensor("out", (N, D), F32, kind="ExternalOutput").ap()
    acc = nc.dram_tensor("acc", (N, D), F32, kind="Internal").ap()
    counts = nc.dram_tensor("counts", (NT, TP, N), F32, kind="Internal").ap()
    gps_block(nc, *aps, acc, counts, out)
    r = run_bass_kernel_spmd(nc, [ins], core_ids=[0])
    return r.results[0]["out"]
```
